# Optimizing a Trainium2 kernel written in Bass

```python
import numpy as np
import jax
import jax.numpy as jnp

def _softmax(x, axis=-1):
    return jax.nn.softmax(x, axis=axis)
def _gelu(x):
    return jax.nn.gelu(x, approximate=True)
def _silu(x):
    return jax.nn.silu(x)
def _sigmoid(x):
    return jax.nn.sigmoid(x)
def _layernorm(x, axis=-1, eps=1e-5):
    m = jnp.mean(x, axis=axis, keepdims=True)
    v = jnp.var(x, axis=axis, keepdims=True)
    return (x - m) / jnp.sqrt(v + eps)
def _scatter_add(tgt, idx, src, axis=0):
    return tgt.at[idx].add(src)
def _segment_sum(src, seg, n):
    return jax.ops.segment_sum(src, seg, n)

kernel_name = 'mk_conv_seq_d2_conv_nchw64_31bdec'

def setup_inputs(seed: int = 0):
    np.random.seed(seed)
    _w = jnp.asarray
    def _rec_inputs():
        import jax
        import jax.numpy as jnp
        _gk = jax.random.key(seed)
        x = -0.0002928 + 1 * jax.random.normal(jax.random.fold_in(_gk, 1), (16, 64, 64, 64), jnp.float32)
        return x
    x = _rec_inputs()
    def _L0_conv_setup():
        import jax, jax.numpy as jnp
        import numpy as np
        B, C, H, W = (16, 64, 64, 64)

        def _maxpool2(y):
            b, c, h, w = y.shape
            return y.reshape(b, c, h // 2, 2, w // 2, 2).max(axis=(3, 5))
        key = jax.random.key(seed)
        ks = jax.random.split(key, 5)
        c8, c2 = (C // 8, C // 2)
        x = jax.random.normal(ks[0], (B, C, H, W), dtype=jnp.float32)
        w_theta = jax.random.normal(ks[1], (c8, C), dtype=jnp.float32) / np.sqrt(C)
        w_phi = jax.random.normal(ks[2], (c8, C), dtype=jnp.float32) / np.sqrt(C)
        w_g = jax.random.normal(ks[3], (c2, C), dtype=jnp.float32) / np.sqrt(C)
        w_o = jax.random.normal(ks[4], (C, c2), dtype=jnp.float32) / np.sqrt(c2)
        gamma = jnp.float32(0.1)
        return {'x': x, 'w_theta': w_theta, 'w_phi': w_phi, 'w_g': w_g, 'w_o': w_o, 'gamma': gamma}
    _L0_conv_all = _L0_conv_setup()
    _L0_conv_in = {k: v for k, v in _L0_conv_all.items() if k in ('w_theta', 'w_phi', 'w_g', 'w_o', 'gamma', )}
    del _L0_conv_all

    def _L1_conv_setup():
        import jax, jax.numpy as jnp
        import numpy as np
        from jax import lax
        C = 64
        EPS = 1e-05

        def conv3x3(x, w):
            return lax.conv_general_dilated(x, w, (1, 1), 'SAME', dimension_numbers=('NCHW', 'OIHW', 'NCHW'))

        def bn_relu(x, g, b, m, v):
            scale = g / jnp.sqrt(v + EPS)
            y = (x - m[None, :, None, None]) * scale[None, :, None, None] + b[None, :, None, None]
            return jax.nn.relu(y)

        def pam(x, wq, bq, wk, bk, wv, bv, gamma):
            N, Cc, H, W = x.shape
            L = H * W
            xf = x.reshape(N, Cc, L)
            q = jnp.einsum('oc,ncl->nlo', wq, xf) + bq
            k = jnp.einsum('oc,ncl->nol', wk, xf) + bk[:, None]
            energy = jnp.einsum('nlo,nom->nlm', q, k)
            attn = jax.nn.softmax(energy, axis=-1)
            v = jnp.einsum('oc,ncl->nol', wv, xf) + bv[:, None]
            out = jnp.einsum('ncm,nlm->ncl', v, attn).reshape(N, Cc, H, W)
            return gamma * out + x

        def cam(x, gamma):
            N, Cc, H, W = x.shape
            xf = x.reshape(N, Cc, H * W)
            energy = jnp.einsum('ncl,ndl->ncd', xf, xf)
            energy = jnp.max(energy, axis=-1, keepdims=True) - energy
            attn = jax.nn.softmax(energy, axis=-1)
            out = jnp.einsum('ncd,ndl->ncl', attn, xf).reshape(N, Cc, H, W)
            return gamma * out + x
        key = jax.random.key(seed)
        ks = jax.random.split(key, 24)
        d = {}
        d['x'] = jax.random.normal(ks[0], (4, C, 64, 64), dtype=jnp.float32)
        s = 0.05
        for i, name in enumerate(['pam1', 'cam1', 'pam2', 'cam2']):
            d['w_' + name] = jax.random.normal(ks[1 + i], (C, C, 3, 3), dtype=jnp.float32) * s
            d['bn_%s_g' % name] = jnp.ones((C,), jnp.float32)
            d['bn_%s_b' % name] = jnp.zeros((C,), jnp.float32)
            d['bn_%s_m' % name] = jnp.zeros((C,), jnp.float32)
            d['bn_%s_v' % name] = jnp.ones((C,), jnp.float32)
        d['wq'] = jax.random.normal(ks[10], (C // 8, C), jnp.float32) * s
        d['bq'] = jnp.zeros((C // 8,), jnp.float32)
        d['wk'] = jax.random.normal(ks[11], (C // 8, C), jnp.float32) * s
        d['bk'] = jnp.zeros((C // 8,), jnp.float32)
        d['wv'] = jax.random.normal(ks[12], (C, C), jnp.float32) * s
        d['bv'] = jnp.zeros((C,), jnp.float32)
        d['gamma_pa'] = jnp.zeros((1,), jnp.float32) + 0.5
        d['gamma_ca'] = jnp.zeros((1,), jnp.float32) + 0.5
        d['w_out'] = jax.random.normal(ks[13], (C, C), jnp.float32) * s
        d['b_out'] = jnp.zeros((C,), jnp.float32)
        return d
    _L1_conv_all = _L1_conv_setup()
    _L1_conv_in = {k: v for k, v in _L1_conv_all.items() if k in ('w_pam1', 'bn_pam1_g', 'bn_pam1_b', 'bn_pam1_m', 'bn_pam1_v', 'w_cam1', 'bn_cam1_g', 'bn_cam1_b', 'bn_cam1_m', 'bn_cam1_v', 'w_pam2', 'bn_pam2_g', 'bn_pam2_b', 'bn_pam2_m', 'bn_pam2_v', 'w_cam2', 'bn_cam2_g', 'bn_cam2_b', 'bn_cam2_m', 'bn_cam2_v', 'wq', 'bq', 'wk', 'bk', 'wv', 'bv', 'gamma_pa', 'gamma_ca', 'w_out', 'b_out', )}
    del _L1_conv_all

    return {
        "x": x,
        "L0_conv_w_theta": _L0_conv_in["w_theta"],
        "L0_conv_w_phi": _L0_conv_in["w_phi"],
        "L0_conv_w_g": _L0_conv_in["w_g"],
        "L0_conv_w_o": _L0_conv_in["w_o"],
        "L0_conv_gamma": _L0_conv_in["gamma"],
        "L1_conv_w_pam1": _L1_conv_in["w_pam1"],
        "L1_conv_bn_pam1_g": _L1_conv_in["bn_pam1_g"],
        "L1_conv_bn_pam1_b": _L1_conv_in["bn_pam1_b"],
        "L1_conv_bn_pam1_m": _L1_conv_in["bn_pam1_m"],
        "L1_conv_bn_pam1_v": _L1_conv_in["bn_pam1_v"],
        "L1_conv_w_cam1": _L1_conv_in["w_cam1"],
        "L1_conv_bn_cam1_g": _L1_conv_in["bn_cam1_g"],
        "L1_conv_bn_cam1_b": _L1_conv_in["bn_cam1_b"],
        "L1_conv_bn_cam1_m": _L1_conv_in["bn_cam1_m"],
        "L1_conv_bn_cam1_v": _L1_conv_in["bn_cam1_v"],
        "L1_conv_w_pam2": _L1_conv_in["w_pam2"],
        "L1_conv_bn_pam2_g": _L1_conv_in["bn_pam2_g"],
        "L1_conv_bn_pam2_b": _L1_conv_in["bn_pam2_b"],
        "L1_conv_bn_pam2_m": _L1_conv_in["bn_pam2_m"],
        "L1_conv_bn_pam2_v": _L1_conv_in["bn_pam2_v"],
        "L1_conv_w_cam2": _L1_conv_in["w_cam2"],
        "L1_conv_bn_cam2_g": _L1_conv_in["bn_cam2_g"],
        "L1_conv_bn_cam2_b": _L1_conv_in["bn_cam2_b"],
        "L1_conv_bn_cam2_m": _L1_conv_in["bn_cam2_m"],
        "L1_conv_bn_cam2_v": _L1_conv_in["bn_cam2_v"],
        "L1_conv_wq": _L1_conv_in["wq"],
        "L1_conv_bq": _L1_conv_in["bq"],
        "L1_conv_wk": _L1_conv_in["wk"],
        "L1_conv_bk": _L1_conv_in["bk"],
        "L1_conv_wv": _L1_conv_in["wv"],
        "L1_conv_bv": _L1_conv_in["bv"],
        "L1_conv_gamma_pa": _L1_conv_in["gamma_pa"],
        "L1_conv_gamma_ca": _L1_conv_in["gamma_ca"],
        "L1_conv_w_out": _L1_conv_in["w_out"],
        "L1_conv_b_out": _L1_conv_in["b_out"],
    }

def reference(x, L0_conv_w_theta, L0_conv_w_phi, L0_conv_w_g, L0_conv_w_o, L0_conv_gamma, L1_conv_w_pam1, L1_conv_bn_pam1_g, L1_conv_bn_pam1_b, L1_conv_bn_pam1_m, L1_conv_bn_pam1_v, L1_conv_w_cam1, L1_conv_bn_cam1_g, L1_conv_bn_cam1_b, L1_conv_bn_cam1_m, L1_conv_bn_cam1_v, L1_conv_w_pam2, L1_conv_bn_pam2_g, L1_conv_bn_pam2_b, L1_conv_bn_pam2_m, L1_conv_bn_pam2_v, L1_conv_w_cam2, L1_conv_bn_cam2_g, L1_conv_bn_cam2_b, L1_conv_bn_cam2_m, L1_conv_bn_cam2_v, L1_conv_wq, L1_conv_bq, L1_conv_wk, L1_conv_bk, L1_conv_wv, L1_conv_bv, L1_conv_gamma_pa, L1_conv_gamma_ca, L1_conv_w_out, L1_conv_b_out):
    import jax
    import jax.numpy as jnp
    def _L0_conv_ref(x, w_theta, w_phi, w_g, w_o, gamma):
        import jax, jax.numpy as jnp
        import numpy as np
        B, C, H, W = (16, 64, 64, 64)

        def _maxpool2(y):
            b, c, h, w = y.shape
            return y.reshape(b, c, h // 2, 2, w // 2, 2).max(axis=(3, 5))
        b, c, h, w = x.shape
        c8, c2 = (c // 8, c // 2)
        s, s4 = (h * w, h * w // 4)
        theta = jnp.einsum('oc,bchw->bohw', w_theta, x).reshape(b, c8, s)
        phi = _maxpool2(jnp.einsum('oc,bchw->bohw', w_phi, x)).reshape(b, c8, s4)
        g = _maxpool2(jnp.einsum('oc,bchw->bohw', w_g, x)).reshape(b, c2, s4)
        beta = jax.nn.softmax(jnp.einsum('bcs,bct->bst', theta, phi), axis=-1)
        o = jnp.einsum('bct,bst->bcs', g, beta).reshape(b, c2, h, w)
        o = jnp.einsum('oc,bchw->bohw', w_o, o)
        return gamma * o + x

    def _L1_conv_ref(x, w_pam1, bn_pam1_g, bn_pam1_b, bn_pam1_m, bn_pam1_v, w_cam1, bn_cam1_g, bn_cam1_b, bn_cam1_m, bn_cam1_v, w_pam2, bn_pam2_g, bn_pam2_b, bn_pam2_m, bn_pam2_v, w_cam2, bn_cam2_g, bn_cam2_b, bn_cam2_m, bn_cam2_v, wq, bq, wk, bk, wv, bv, gamma_pa, gamma_ca, w_out, b_out):
        import jax, jax.numpy as jnp
        import numpy as np
        from jax import lax
        C = 64
        EPS = 1e-05

        def conv3x3(x, w):
            return lax.conv_general_dilated(x, w, (1, 1), 'SAME', dimension_numbers=('NCHW', 'OIHW', 'NCHW'))

        def bn_relu(x, g, b, m, v):
            scale = g / jnp.sqrt(v + EPS)
            y = (x - m[None, :, None, None]) * scale[None, :, None, None] + b[None, :, None, None]
            return jax.nn.relu(y)

        def pam(x, wq, bq, wk, bk, wv, bv, gamma):
            N, Cc, H, W = x.shape
            L = H * W
            xf = x.reshape(N, Cc, L)
            q = jnp.einsum('oc,ncl->nlo', wq, xf) + bq
            k = jnp.einsum('oc,ncl->nol', wk, xf) + bk[:, None]
            energy = jnp.einsum('nlo,nom->nlm', q, k)
            attn = jax.nn.softmax(energy, axis=-1)
            v = jnp.einsum('oc,ncl->nol', wv, xf) + bv[:, None]
            out = jnp.einsum('ncm,nlm->ncl', v, attn).reshape(N, Cc, H, W)
            return gamma * out + x

        def cam(x, gamma):
            N, Cc, H, W = x.shape
            xf = x.reshape(N, Cc, H * W)
            energy = jnp.einsum('ncl,ndl->ncd', xf, xf)
            energy = jnp.max(energy, axis=-1, keepdims=True) - energy
            attn = jax.nn.softmax(energy, axis=-1)
            out = jnp.einsum('ncd,ndl->ncl', attn, xf).reshape(N, Cc, H, W)
            return gamma * out + x
        p = bn_relu(conv3x3(x, w_pam1), bn_pam1_g, bn_pam1_b, bn_pam1_m, bn_pam1_v)
        p = pam(p, wq, bq, wk, bk, wv, bv, gamma_pa)
        p = bn_relu(conv3x3(p, w_pam2), bn_pam2_g, bn_pam2_b, bn_pam2_m, bn_pam2_v)
        c = bn_relu(conv3x3(x, w_cam1), bn_cam1_g, bn_cam1_b, bn_cam1_m, bn_cam1_v)
        c = cam(c, gamma_ca)
        c = bn_relu(conv3x3(c, w_cam2), bn_cam2_g, bn_cam2_b, bn_cam2_m, bn_cam2_v)
        feat = p + c
        out = jnp.einsum('oc,nchw->nohw', w_out, feat) + b_out[None, :, None, None]
        return out

    def _gn(v, G=32, eps=1e-5):
        B_, C_, H_, W_ = v.shape
        g = v.reshape(B_, G, C_ // G, H_, W_)
        m = jnp.mean(g, axis=(2, 3, 4), keepdims=True)
        s = jnp.var(g, axis=(2, 3, 4), keepdims=True)
        return ((g - m) / jnp.sqrt(s + eps)).reshape(v.shape)

    def _ln_c(v, eps=1e-6):
        m = jnp.mean(v, axis=1, keepdims=True)
        s = jnp.var(v, axis=1, keepdims=True)
        return (v - m) / jnp.sqrt(s + eps)

    def _ln_t(v, eps=1e-5):
        m = jnp.mean(v, axis=-1, keepdims=True)
        s = jnp.var(v, axis=-1, keepdims=True)
        return (v - m) / jnp.sqrt(s + eps)

    def _to_tokens(v):
        B_, C_, H_, W_ = v.shape
        return v.reshape(B_, C_, H_ * W_).transpose(0, 2, 1)
    def _from_tokens(t, like):
        B_, C_, H_, W_ = like.shape
        return t.transpose(0, 2, 1).reshape(B_, C_, H_, W_)

    x = _L0_conv_ref(x, L0_conv_w_theta, L0_conv_w_phi, L0_conv_w_g, L0_conv_w_o, L0_conv_gamma)
    x = _L1_conv_ref(x, L1_conv_w_pam1, L1_conv_bn_pam1_g, L1_conv_bn_pam1_b, L1_conv_bn_pam1_m, L1_conv_bn_pam1_v, L1_conv_w_cam1, L1_conv_bn_cam1_g, L1_conv_bn_cam1_b, L1_conv_bn_cam1_m, L1_conv_bn_cam1_v, L1_conv_w_pam2, L1_conv_bn_pam2_g, L1_conv_bn_pam2_b, L1_conv_bn_pam2_m, L1_conv_bn_pam2_v, L1_conv_w_cam2, L1_conv_bn_cam2_g, L1_conv_bn_cam2_b, L1_conv_bn_cam2_m, L1_conv_bn_cam2_v, L1_conv_wq, L1_conv_bq, L1_conv_wk, L1_conv_bk, L1_conv_wv, L1_conv_bv, L1_conv_gamma_pa, L1_conv_gamma_ca, L1_conv_w_out, L1_conv_b_out)
    return x


_drawn_inputs = setup_inputs


def setup_inputs(seed=0):
    import zlib

    import numpy as np

    out = dict(_drawn_inputs(seed))
    spreads = {'L1_conv_bn_pam1_g': (1.0, 0.2),
     'L1_conv_bn_pam1_b': (0.0, 0.1),
     'L1_conv_bn_pam1_m': (0.0, 0.1),
     'L1_conv_bn_pam1_v': (1.0, 0.2),
     'L1_conv_bn_cam1_g': (1.0, 0.2),
     'L1_conv_bn_cam1_b': (0.0, 0.1),
     'L1_conv_bn_cam1_m': (0.0, 0.1),
     'L1_conv_bn_cam1_v': (1.0, 0.2),
     'L1_conv_bn_pam2_g': (1.0, 0.2),
     'L1_conv_bn_pam2_b': (0.0, 0.1),
     'L1_conv_bn_pam2_m': (0.0, 0.1),
     'L1_conv_bn_pam2_v': (1.0, 0.2),
     'L1_conv_bn_cam2_g': (1.0, 0.2),
     'L1_conv_bn_cam2_b': (0.0, 0.1),
     'L1_conv_bn_cam2_m': (0.0, 0.1),
     'L1_conv_bn_cam2_v': (1.0, 0.2),
     'L1_conv_bq': (0.0, 0.8),
     'L1_conv_bk': (0.0, 0.8),
     'L1_conv_bv': (0.0, 0.316),
     'L1_conv_b_out': (0.0, 0.1)}
    factors = {'L1_conv_wq': 8.0, 'L1_conv_wk': 8.0}
    for name, (base, spread) in spreads.items():
        noise = np.random.default_rng([zlib.crc32(name.encode()), seed]).standard_normal(out[name].shape)
        drawn = base * np.exp(spread * noise) if base else spread * noise
        out[name] = jnp.asarray(drawn.astype(out[name].dtype))
    for name, factor in factors.items():
        out[name] = (out[name] * factor).astype(out[name].dtype)
    return out
```

```python
from contextlib import ExitStack

import concourse.bass as bass
from concourse import mybir

ALU = mybir.AluOpType
ACT = mybir.ActivationFunctionType
AX = mybir.AxisListType
F32 = mybir.dt.float32
F32R = mybir.dt.float32r

B, C, H, W = 16, 64, 64, 64
L = H * W
P = 128
CHUNK = 512
NCH = L // CHUNK
ROWS = CHUNK // W
QT = CHUNK // P
HP, WP = H + 2, W + 2
TAPS = 9
C8, C2 = C // 8, C // 2
KEYS = (L // 4, L)
TILES = (KEYS[0] // P, KEYS[1] // P)
TILE_OFF = (0, TILES[0] * NCH)
TILES_ALL = (TILES[0] + TILES[1]) * NCH
STEPS = 2 * NCH
LAG = 3
POST_SLOT = (4, 8)
ROW_SLOT = (6, 27)
(BN1_G, BN1_B, BN1_M, BN1_V, BN2_G, BN2_B, BN2_M, BN2_V, B_QK, B_V, B_OUT, GAMMA0, GAMMA_PA, GAMMA_CA,
 MASK_HALF, MASK_QK, MASK_ROW) = range(17)
NCOL = 17


def units_at(layer, t):
    n = TILES[layer]
    at = [min(n, 2 * s) for s in range(n + 1)] if layer == 0 else [min(n, (4 * s) // 3) for s in range(n + 1)]
    return range(at[t], at[t + 1])


def last_units(layer):
    return max(t for t in range(TILES[layer]) if len(units_at(layer, t)))


def build(nc, x, cols, ident, w_in0, w_o0, w_qk, w_v, w_c1, w_c2p, w_c2c, w_out, out):
    ctx = ExitStack()
    with ctx:
        def sb(name, shape, dt=F32):
            return ctx.enter_context(nc.sbuf_tensor(name, shape, dt))

        def sem(name):
            return ctx.enter_context(nc.semaphore(name))

        work = ctx.enter_context(nc.psum_tensor("work", [P, 4, CHUNK], F32))
        smax = ctx.enter_context(nc.psum_tensor("smax", [P, 2, CHUNK], F32))
        wsum = ctx.enter_context(nc.psum_tensor("wsum", [P, CHUNK], F32))
        post = ctx.enter_context(nc.psum_tensor("post", [P, CHUNK], F32))

        col = sb("col", [P, NCOL])
        idn = sb("idn", [P, P])
        neg_idn = sb("neg_idn", [P, P])
        two_idn = sb("two_idn", [P, P])
        wi0 = sb("wi0", [C, P])
        proj_y = sb("proj_y", [96, P])
        proj_p = sb("proj_p", [P, P])
        wqk = sb("wqk", [C, C])
        w1 = sb("w1", [P, 2, TAPS, P], F32R)
        w2p = sb("w2p", [P, TAPS, P], F32R)
        w2c = sb("w2c", [P, TAPS, P], F32R)
        wout = sb("wout", [P, C])
        bn = sb("bn", [P, 2, 6])
        bqk_m = sb("bqk_m", [C, 1])
        bv_g = sb("bv_g", [P, 2])

        x_in = sb("x_in", [96, L])
        y_pad = sb("y_pad", [P, HP, WP], F32R)
        c_pad = sb("c_pad", [P, HP, WP], F32R)
        pc = sb("pc", [P, L])
        pt_ct = sb("pt_ct", [P, TILES[1], 3 * C])
        gt = sb("gt", [P, TILES[0], 96])
        keys = sb("keys", [C, L], F32R)
        qall = sb("qall", [32, L])
        qs = sb("qs", [C, 2, CHUNK], F32R)
        pooled = sb("pooled", [P, KEYS[0]])
        probs = sb("probs", [P, 4, CHUNK])
        ones = sb("ones", [32, CHUNK])
        sums = sb("sums", [P, CHUNK])
        inv_t = sb("inv_t", [C, CHUNK])
        inv_c = sb("inv_c", [P, CHUNK // 32])
        inv = sb("inv", [P, CHUNK])
        mx = sb("mx", [P, 2, QT, 8])
        mx1 = sb("mx1", [P, 2, QT])
        row_coarse = sb("row_coarse", [32, CHUNK])
        coarse = sb("coarse", [P, 2, CHUNK])
        part = sb("part", [P, 2, CHUNK])
        bsum = sb("bsum", [P, 2, CHUNK])
        ostage = sb("ostage", [C, 2, CHUNK])
        en = sb("en", [C, C])
        ex = sb("ex", [C, C])
        attn = sb("attn", [C, 2, C])
        cam_w = sb("cam_w", [P, P])
        st = sb("st", [C, 6])
        wtmp = pc

        consts_in = sem("consts_in")
        consts_ready = sem("consts_ready")
        setup_act = sem("setup_act")
        setup_dve = sem("setup_dve")
        x_loaded = sem("x_loaded")
        in0_ready = sem("in0_ready")
        theta_coarse = sem("theta_coarse")
        in0_used = sem("in0_used")
        phi_coarse = sem("phi_coarse")
        pool_done = sem("pool_done")
        phi_split = sem("phi_split")
        gt_ready = sem("gt_ready")
        gt_copied = sem("gt_copied")
        staged = sem("staged")
        smax_ready = sem("smax_ready")
        max_done = sem("max_done")
        mx_ready = sem("mx_ready")
        row_ready = sem("row_ready")
        row_coarse_ready = sem("row_coarse_ready")
        row_split = sem("row_split")
        scores_ready = sem("scores_ready")
        exp_done = sem("exp_done")
        probs_used = sem("probs_used")
        sums_copied = sem("sums_copied")
        norm_step = sem("norm_step")
        u_ready = sem("u_ready")
        post_ready = sem("post_ready")
        post_coarse = sem("post_coarse")
        post_split = sem("post_split")
        conv1_ready = sem("conv1_ready")
        pc_ready = sem("pc_ready")
        tr_ready = sem("tr_ready")
        tr_copied = sem("tr_copied")
        energy_ready = sem("energy_ready")
        cam_step = sem("cam_step")
        cam_exp = sem("cam_exp")
        attn_ready = sem("attn_ready")
        attn_t_ready = sem("attn_t_ready")
        cam_w_ready = sem("cam_w_ready")
        qk_ready = sem("qk_ready")
        qk_coarse = sem("qk_coarse")
        qk_split = sem("qk_split")
        cam_ready = sem("cam_ready")
        cam_coarse = sem("cam_coarse")
        cam_split = sem("cam_split")
        conv2_ready = sem("conv2_ready")
        part_ready = sem("part_ready")
        branch_sum = sem("branch_sum")
        feat_ready = sem("feat_ready")
        out_ready = sem("out_ready")
        out_staged = sem("out_staged")
        out_stored = [sem(f"out_stored{i}") for i in range(2)]

        def tile_no(b, layer, c, t):
            return b * TILES_ALL + c * TILES[layer] + (TILE_OFF[layer] + t)

        def step_no(b, layer, c):
            return b * STEPS + (c + NCH * layer)

        def chunk(c):
            return bass.ds(c * CHUNK, CHUNK)

        def image_rows(tile, c, half=slice(0, P)):
            return tile[half, bass.ds(c * ROWS + 1, ROWS), 1:1 + W]

        def chunk_loop(eng, step):
            step(0, 0, True, False)
            with eng.Fori(0, NCH // 2 - 1) as turn:
                step(turn * 2 + 1, 1, False, False)
                step(turn * 2 + 2, 0, False, False)
            step(NCH - 1, 1, False, True)

        def settle(eng):
            eng.wait_ge(consts_ready, 1)

        block = ctx.enter_context(nc.Block())

        @block.sync
        def _(sp):
            loads = [(col[:], cols), (idn[:], ident), (two_idn[0:C, 0:C], ident[0:C, 0:C]),
                     (two_idn[0:C, C:P], ident[0:C, 0:C]), (two_idn[C:P, 0:C], ident[0:C, 0:C]),
                     (two_idn[C:P, C:P], ident[0:C, 0:C]), (wi0[:], w_in0), (proj_y[C:96, :], w_o0),
                     (proj_p[C:P, :], w_v), (wqk[:], w_qk), (wtmp[:, 0:TAPS * P], w_c1),
                     (wtmp[:, TAPS * P:TAPS * (P + C)], w_c2p), (wtmp[:, TAPS * (P + C):TAPS * 2 * P], w_c2c),
                     (wout[:], w_out), (proj_y[0:C, 0:C], ident[0:C, 0:C]), (proj_y[0:C, C:P], ident[0:C, 0:C]),
                     (proj_p[0:C, 0:C], ident[0:C, 0:C]), (proj_p[0:C, C:P], ident[0:C, 0:C])]
            assert len(loads) == N_LOADS
            for dst, src in loads:
                sp.dma_start(dst, src).then_inc(consts_in, 16)
            for s in out_stored:
                sp.sem_inc(s, 16)
            sp.dma_start(x_in[0:C, :], x[0]).then_inc(x_loaded, 16)

            def store(b, c, par, first, last):
                sp.wait_ge(out_staged, b * NCH + (c + 1 + 2))
                sp.dma_start(out_view(b, c), ostage[:, par, :]).then_inc(out_stored[par], 16)

            def out_view(b, c):
                return out[bass.ds(b, 1), :, chunk(c)].rearrange("o c l -> (o c) l")

            def stores(b):
                chunk_loop(sp, lambda c, par, first, last: store(b, c, par, first, last))

            with sp.Fori(0, B - 1) as b:
                sp.wait_ge(post_ready, b * STEPS + NCH)
                sp.dma_start(x_in[0:C, :], x[bass.ds(b + 1, 1)].rearrange("o c l -> (o c) l")).then_inc(x_loaded, 16)
                stores(b)
            stores(B - 1)
            for s in out_stored:
                sp.wait_ge(s, 16 + B * NCH // 2 * 16)

        @block.gpsimd
        def _(pool):
            def stage(b, layer, c, par):
                nc.gpsimd.tensor_tensor(qs[0:32, par, :], qall[:, chunk(c)], ones[:, :], ALU.mult).then_inc(staged, 1)

            def wait_alone(semaphore, value):
                settle(pool)
                pool.wait_ge(semaphore, value)

            def layer_stages(b, layer):
                split = (in0_used, qk_split)[layer]
                wait_alone(split, b * NCH + 1)
                stage(b, layer, 0, 0)
                wait_alone(split, b * NCH + NCH)

                def step(c, par, first, last):
                    if last:
                        return
                    if not first:
                        wait_alone(probs_used, tile_no(b, layer, c, 4))
                    stage(b, layer, c + 1, 1 - par)
                chunk_loop(pool, step)

            with pool.Fori(0, B) as b:
                layer_stages(b, 0)
                layer_stages(b, 1)

        @block.tensor
        def _(pe):
            def mm(o, a, r, start=True, stop=True):
                return nc.tensor.matmul(o, a, r, start=start, stop=stop)

            pe.sem_inc(probs_used, 4)
            pe.sem_inc(out_ready, 2)
            pe.wait_ge(consts_ready, 1)

            def max_unit(b, layer, c, par, u, lt, kc):
                pe.wait_ge(max_done, tile_no(b, layer, c, u + 1))
                mm(smax[:, u % 2, :], qs[0:32, par, lt * P:(lt + 1) * P],
                   keys[0:32, kc * CHUNK:(kc + 1) * CHUNK]).then_inc(smax_ready, 1)

            def max_row(b, layer, c, par):
                pe.wait_ge(mx_ready, step_no(b, layer, c) + 1)
                for lt in range(QT):
                    last = mm(post[0:32, lt * P:(lt + 1) * P],
                              mx1[:, par, lt:lt + 1].to_broadcast([P, 32]), neg_idn[:, :])
                last.then_inc(row_ready, 1)

            def project(b, layer, c):
                pe.wait_ge(u_ready, step_no(b, layer, c) + 2)
                if layer == 0:
                    last = mm(post[:, :], proj_y[:, :], x_in[:, chunk(c)])
                else:
                    last = mm(post[:, :], proj_p[:, :], pc[:, chunk(c)])
                last.then_inc(post_ready, 1)

            def weigh(b, layer, c, t):
                n = TILES[layer]
                pe.wait_ge(exp_done, tile_no(b, layer, c, t + 1 + 4))
                if layer == 0:
                    o, a = wsum[0:96, :], gt[:, t, :]
                else:
                    o, a = wsum[:, :], pt_ct[:, t, 0:2 * C]
                mm(o, a, probs[:, t % 4, :], start=(t == 0), stop=(t == n - 1)).then_inc(probs_used, 1)

            def attend(b, layer, c, par, first, last):
                n = TILES[layer]
                pe.wait_ge(row_split, step_no(b, layer, c) + 2)
                for t in range(n + LAG):
                    if t < n:
                        pe.wait_ge(exp_done, tile_no(b, layer, c, t + 1))
                        mm(work[:, t % 4, :], keys[:, t * P:(t + 1) * P], qs[:, par, :]).then_inc(scores_ready, 1)
                        if not last:
                            if t == 0:
                                pe.wait_ge(staged, step_no(b, layer, c) + 2)
                            for u in units_at(layer, t):
                                max_unit(b, layer, c + 1, 1 - par, u, u // (n // QT), u % (n // QT))
                    if t >= LAG:
                        if t == LAG:
                            pe.wait_ge(sums_copied, step_no(b, layer, c) + 1)
                        weigh(b, layer, c, t - LAG)
                    if t == POST_SLOT[layer] and not first:
                        project(b, layer, c - 1)
                    if t == ROW_SLOT[layer] and not last:
                        if not first:
                            pe.wait_ge(post_split, step_no(b, layer, c) + 1)
                        max_row(b, layer, c + 1, 1 - par)

            def proj0(b, c):
                if c >= 2:
                    pe.wait_ge(in0_used, b * NCH + (c - 1))
                mm(work[:, c % 2, :], wi0[:, :], x_in[0:C, chunk(c)]).then_inc(in0_ready, 1)

            def conv1(b, c):
                if c == 0:
                    pe.wait_ge(post_split, step_no(b, 0, NCH - 1) + 1)
                if c == 2:
                    pe.wait_ge(post_split, step_no(b, 0, NCH) + 1)
                if c >= 2:
                    pe.wait_ge(pc_ready, b * NCH + (c - 1))
                for i in range(2 * TAPS):
                    half, tap = divmod(i, TAPS)
                    dy, dx = divmod(tap, 3)
                    last = mm(work[:, c % 2, :], w1[:, half, tap, :],
                              y_pad[:, ROWS * c + dy:ROWS * c + dy + ROWS, dx:dx + W],
                              start=(i == 0), stop=(i == 2 * TAPS - 1))
                last.then_inc(conv1_ready, 1)

            def transposes(b, c):
                pe.wait_ge(pc_ready, b * NCH + c + 1)
                if c >= 1:
                    pe.wait_ge(tr_copied, b * NCH + c)
                for i in range(QT):
                    t = QT * c + i
                    last = nc.tensor.transpose(wsum[:, i * P:(i + 1) * P], pc[:, t * P:(t + 1) * P], idn[:, :])
                last.then_inc(tr_ready, 1)

            def energy(b, c):
                pe.wait_ge(tr_copied, b * NCH + c + 1)
                for i in range(QT):
                    t = QT * c + i
                    ct = pt_ct[:, t, 2 * C:3 * C]
                    last = mm(post[0:C, 0:C], ct, ct, start=(t == 0), stop=(t == TILES[1] - 1))
                if c == NCH - 1:
                    last.then_inc(energy_ready, 1)

            def query_key(b, c):
                if c >= 2:
                    settle(pe)
                    pe.wait_ge(qk_split, b * NCH + (c - 1))
                mm(work[0:C, 2 + c % 2, :], wqk[:, :], pc[0:C, chunk(c)]).then_inc(qk_ready, 1)

            def conv2(b, c, par, first, last):
                if first:
                    pe.wait_ge(post_split, step_no(b, 1, NCH - 1) + 1)
                pe.wait_ge(branch_sum, b * NCH + (c + 1))
                for k, (pad, w) in enumerate(((y_pad, w2p), (c_pad, w2c))):
                    for tap in range(TAPS):
                        dy, dx = divmod(tap, 3)
                        end = mm(work[:, 2 * k + par, :], w[:, tap, :],
                                 pad[:, bass.ds(c * ROWS + dy, ROWS), dx:dx + W],
                                 start=(tap == 0), stop=(tap == TAPS - 1))
                end.then_inc(conv2_ready, 1)
                if first:
                    project(b, 1, NCH - 1)
                    settle(pe)
                    pe.wait_ge(post_split, step_no(b, 1, NCH) + 1)
                else:
                    out_project(b, c - 1, 1 - par)

            def out_project(b, c, par):
                pe.wait_ge(feat_ready, b * NCH + (c + 1 + 2))
                pe.wait_ge(out_staged, b * NCH + (c + 1))
                mm(smax[0:C, par, :], wout[:, :], coarse[:, par, :]).then_inc(out_ready, 1)

            with pe.Fori(0, B) as b:
                pe.wait_ge(x_loaded, b * 16 + 16)
                for c in range(NCH):
                    proj0(b, c)
                pe.wait_ge(out_staged, b * NCH + 2)
                pe.wait_ge(phi_split, b * NCH + NCH)
                pe.wait_ge(staged, step_no(b, 0, 0) + 1)
                for u in range(TILES[0]):
                    max_unit(b, 0, 0, 0, u, u % QT, u // QT)
                settle(pe)
                pe.wait_ge(pool_done, b * NCH + NCH)
                for t in range(TILES[0]):
                    last = nc.tensor.transpose(wsum[:, t * 32:(t + 1) * 32], pooled[96:P, t * P:(t + 1) * P],
                                               idn[96:P, 96:P])
                last.then_inc(gt_ready, 1)
                max_row(b, 0, 0, 0)
                pe.wait_ge(gt_copied, b + 1)
                chunk_loop(pe, lambda c, par, first, last: attend(b, 0, c, par, first, last))

                conv1(b, 0)
                conv1(b, 1)
                project(b, 0, NCH - 1)
                for c in range(2, NCH + 3):
                    if c < NCH:
                        conv1(b, c)
                    if c - 2 < NCH:
                        transposes(b, c - 2)
                        query_key(b, c - 2)
                    if 3 <= c:
                        energy(b, c - 3)
                        if c == 3:
                            pe.wait_ge(staged, step_no(b, 1, 0) + 1)
                        pe.wait_ge(qk_split, b * NCH + (c - 2))
                        for lt in range(QT):
                            max_unit(b, 1, 0, 0, (c - 3) * QT + lt, lt, c - 3)
                pe.wait_ge(attn_ready, b + 1)
                mm(wsum[:, 0:P], attn[:, :, :].rearrange("c a d -> c (a d)"), two_idn[0:C, :]).then_inc(attn_t_ready, 1)
                max_row(b, 1, 0, 0)
                pe.wait_ge(cam_w_ready, b + 1)
                for c in range(NCH):
                    if c >= 2:
                        pe.wait_ge(cam_split, b * NCH + (c - 1))
                    mm(work[:, c % 2, :], cam_w[C:P, :], pc[C:P, chunk(c)]).then_inc(cam_ready, 1)
                pe.wait_ge(cam_split, b * NCH + NCH)
                chunk_loop(pe, lambda c, par, first, last: attend(b, 1, c, par, first, last))
                chunk_loop(pe, lambda c, par, first, last: conv2(b, c, par, first, last))
                out_project(b, NCH - 1, 1)

        @block.scalar
        def _(act):
            def affine(o, i, scale=1.0, bias=0.0):
                return nc.scalar.activation(o, i, ACT.Identity, bias=bias, scale=scale)

            act.sem_inc(exp_done, 4)
            act.sem_inc(sums_copied, 1)
            act.sem_inc(feat_ready, 2)
            act.wait_ge(setup_dve, 1)
            for k in range(2):
                nc.scalar.activation(bn[:, k, 1:2], bn[:, k, 0:1], ACT.Sqrt).then_inc(setup_act, 1)
            act.wait_ge(consts_ready, 1)

            def copy_sums(b, layer, c):
                n = 96 if layer == 0 else P
                act.wait_ge(probs_used, tile_no(b, layer, c + 1, 4))
                act.wait_ge(u_ready, step_no(b, layer, c) + 1)
                nc.scalar.copy(sums[0:n, :], wsum[0:n, :]).then_inc(sums_copied, 1)

            def split_post(b, layer, c):
                act.wait_ge(post_ready, step_no(b, layer, c) + 1)
                act.wait_ge(post_split, step_no(b, layer, c) + 1)
                o = coarse[:, 0, :].bitcast(F32R)
                if layer == 0:
                    affine(o, post[:, :], scale=col[:, MASK_HALF:MASK_HALF + 1]).then_inc(post_coarse, 1)
                else:
                    affine(o, post[:, :], scale=col[:, MASK_HALF:MASK_HALF + 1],
                           bias=bv_g[:, 1:2]).then_inc(post_coarse, 1)

            def split_row(b, layer, c):
                act.wait_ge(row_ready, step_no(b, layer, c) + 1)
                act.wait_ge(row_split, step_no(b, layer, c) + 1)
                affine(row_coarse[:, :].bitcast(F32R), post[0:32, :],
                       scale=col[0:32, MASK_ROW:MASK_ROW + 1]).then_inc(row_coarse_ready, 1)

            def attend(b, layer, c, par, first, last):
                n = TILES[layer]
                for t in range(n):
                    act.wait_ge(scores_ready, tile_no(b, layer, c, t + 1))
                    act.wait_ge(probs_used, tile_no(b, layer, c, t + 1))
                    nc.scalar.activation(probs[:, t % 4, :], work[:, t % 4, :], ACT.Exp).then_inc(exp_done, 1)
                    if t == 1 and not first:
                        copy_sums(b, layer, c - 1)
                    if t == POST_SLOT[layer] + 1 and not first:
                        split_post(b, layer, c - 1)
                    if t == ROW_SLOT[layer] + 1 and not last:
                        split_row(b, layer, c + 1)

            def conv1_out(b, c):
                act.wait_ge(conv1_ready, b * NCH + c + 1)
                nc.scalar.activation(pc[:, chunk(c)], work[:, c % 2, :], ACT.Relu, bias=bn[:, 0, 5:6],
                                     scale=bn[:, 0, 4:5]).then_inc(pc_ready, 1)

            def qk_out(b, c):
                act.wait_ge(qk_ready, b * NCH + c + 1)
                if c >= 2:
                    act.wait_ge(qk_split, b * NCH + (c - 1))
                affine(coarse[0:C, c % 2, :].bitcast(F32R), work[0:C, 2 + c % 2, :],
                       scale=col[0:C, MASK_QK:MASK_QK + 1], bias=bqk_m[:, :]).then_inc(qk_coarse, 1)

            def conv2_out(b, c, par, first, last):
                act.wait_ge(conv2_ready, b * NCH + (c + 1))
                act.wait_ge(branch_sum, b * NCH + (c + 1))
                nc.scalar.copy(part[0:C, par, :], work[C:P, par, :])
                nc.scalar.copy(part[C:P, par, :], work[0:C, 2 + par, :]).then_inc(part_ready, 1)
                if first:
                    split_post(b, 1, NCH - 1)
                    act.wait_ge(post_split, step_no(b, 1, NCH) + 1)
                else:
                    features(b, c - 1, 1 - par)

            def features(b, c, par):
                act.wait_ge(branch_sum, b * NCH + (c + 1 + 2))
                act.wait_ge(out_ready, b * NCH + (c + 1))
                nc.scalar.activation(coarse[:, par, :], bsum[:, par, :], ACT.Relu, bias=bn[:, 1, 5:6],
                                     scale=bn[:, 1, 4:5]).then_inc(feat_ready, 1)

            with act.Fori(0, B) as b:
                for c in range(NCH):
                    act.wait_ge(in0_ready, b * NCH + c + 1)
                    if c >= 2:
                        act.wait_ge(in0_used, b * NCH + (c - 1))
                    if c == 0:
                        act.wait_ge(out_ready, b * NCH + 2)
                    affine(coarse[0:32, c % 2, :].bitcast(F32R), work[0:32, c % 2, :],
                           scale=col[0:32, MASK_QK:MASK_QK + 1]).then_inc(theta_coarse, 1)
                    act.wait_ge(pool_done, b * NCH + c + 1)
                    affine(part[C:96, c % 2, 0:P].bitcast(F32R), pooled[C:96, c * P:(c + 1) * P],
                           scale=col[C:96, MASK_QK:MASK_QK + 1]).then_inc(phi_coarse, 1)
                split_row(b, 0, 0)
                chunk_loop(act, lambda c, par, first, last: attend(b, 0, c, par, first, last))
                copy_sums(b, 0, NCH - 1)
                conv1_out(b, 0)
                conv1_out(b, 1)
                split_post(b, 0, NCH - 1)
                act.wait_ge(post_split, step_no(b, 0, NCH) + 1)
                for c in range(2, NCH + 2):
                    if c < NCH:
                        conv1_out(b, c)
                    qk_out(b, c - 2)
                act.wait_ge(cam_step, b * 5 + 4)
                nc.scalar.activation(ex[:, :], en[:, :], ACT.Exp, bias=st[:, 2:3],
                                     accum_out=st[:, 3:4]).then_inc(cam_exp, 1)
                split_row(b, 1, 0)
                for c in range(NCH):
                    act.wait_ge(cam_ready, b * NCH + c + 1)
                    if c >= 2:
                        act.wait_ge(cam_split, b * NCH + (c - 1))
                    else:
                        act.wait_ge(qk_split, b * NCH + NCH)
                    affine(coarse[:, c % 2, :].bitcast(F32R), work[:, c % 2, :],
                           scale=col[:, MASK_HALF:MASK_HALF + 1]).then_inc(cam_coarse, 1)
                act.wait_ge(cam_split, b * NCH + NCH)
                chunk_loop(act, lambda c, par, first, last: attend(b, 1, c, par, first, last))
                copy_sums(b, 1, NCH - 1)
                chunk_loop(act, lambda c, par, first, last: conv2_out(b, c, par, first, last))
                features(b, NCH - 1, 1)

        @block.vector
        def _(dve):
            v = nc.vector
            dve.sem_inc(max_done, 2)
            dve.sem_inc(row_split, 1)
            dve.sem_inc(u_ready, 1)
            dve.sem_inc(post_split, 1)
            dve.sem_inc(branch_sum, 2)
            dve.sem_inc(out_staged, 2)
            dve.wait_ge(consts_in, 16 * N_LOADS)
            n_setup = 0

            def link(ins):
                nonlocal n_setup
                n_setup += 1
                ins.then_inc(setup_dve, 1)
                dve.wait_ge(setup_dve, n_setup)

            for k, (g, bb, m, var) in enumerate(((BN1_G, BN1_B, BN1_M, BN1_V), (BN2_G, BN2_B, BN2_M, BN2_V))):
                ins = v.tensor_scalar(bn[:, k, 0:1], col[:, var:var + 1], 1e-5, None, ALU.add)
            link(ins)
            dve.wait_ge(setup_act, 2)
            for k, (g, bb, m, var) in enumerate(((BN1_G, BN1_B, BN1_M, BN1_V), (BN2_G, BN2_B, BN2_M, BN2_V))):
                q = [bn[:, k, i:i + 1] for i in range(6)]
                link(v.reciprocal(q[2], q[1]))
                link(v.tensor_tensor(q[3], q[0], q[2], ALU.mult))
                link(v.tensor_tensor(q[3], q[3], q[1], ALU.add))
                link(v.tensor_scalar(q[3], q[3], 0.5, None, ALU.mult))
                link(v.reciprocal(q[2], q[3]))
                link(v.tensor_tensor(q[4], q[2], col[:, g:g + 1], ALU.mult))
                link(v.tensor_tensor(q[3], q[4], col[:, m:m + 1], ALU.mult))
                link(v.tensor_tensor(q[5], col[:, bb:bb + 1], q[3], ALU.subtract))
            v.tensor_scalar(neg_idn[:], idn[:], -1.0, None, ALU.mult)
            v.tensor_scalar(proj_y[C:96, :], proj_y[C:96, :], col[C:96, GAMMA0:GAMMA0 + 1], None, ALU.mult)
            v.tensor_scalar(proj_p[C:P, :], proj_p[C:P, :], col[C:P, GAMMA_PA:GAMMA_PA + 1], None, ALU.mult)
            link(v.tensor_tensor(bv_g[:, 0:1], col[:, B_V:B_V + 1], col[:, GAMMA_PA:GAMMA_PA + 1], ALU.mult))
            v.tensor_tensor(bv_g[:, 1:2], bv_g[:, 0:1], col[:, MASK_HALF:MASK_HALF + 1], ALU.mult)
            v.tensor_tensor(bqk_m[:, :], col[0:C, B_QK:B_QK + 1], col[0:C, MASK_QK:MASK_QK + 1], ALU.mult)
            c1 = wtmp[:, 0:TAPS * P].rearrange("p (t m) -> p t m", t=TAPS)
            link(v.tensor_copy(w1[:, 0, :, :], c1))
            link(v.tensor_tensor(w1[:, 1, :, :], c1, w1[:, 0, :, :].bitcast(F32), ALU.subtract))
            for w, off, hi in ((w2p, TAPS * P, 0), (w2c, TAPS * (P + C), 1)):
                src = wtmp[:, off:off + TAPS * C].rearrange("p (t m) -> p t m", t=TAPS)
                a, f = w[:, :, hi * C:(hi + 1) * C], w[:, :, (1 - hi) * C:(2 - hi) * C]
                link(v.tensor_copy(a, src))
                link(v.tensor_tensor(f, src, a.bitcast(F32), ALU.subtract))
            v.memset(y_pad[:].bitcast(F32), 0.0)
            v.memset(c_pad[:].bitcast(F32), 0.0)
            v.memset(keys[32:C, :].bitcast(F32), 0.0)
            v.memset(pt_ct[:, :, 0:C], 1.0)
            v.memset(ones[:, :], 1.0)
            link(v.memset(gt[:, :, 0:C], 1.0))
            v.memset(keys[32:34, :].bitcast(F32), 1.0).then_inc(consts_ready, 1)

            def take_max(b, layer, c, par, u, lt, kc):
                dve.wait_ge(smax_ready, tile_no(b, layer, c, u + 1))
                v.tensor_reduce(mx[:, par, lt, kc:kc + 1], smax[:, u % 2, :], AX.X, ALU.max).then_inc(max_done, 1)

            def finish_max(b, layer, c, par):
                n = TILES[layer] // QT
                dve.wait_ge(max_done, tile_no(b, layer, c + 1, 2))
                v.tensor_reduce(mx1[:, par, :], mx[:, par, :, 0:n], AX.X, ALU.max).then_inc(mx_ready, 1)

            def split_row(b, layer, c, par):
                dve.wait_ge(row_coarse_ready, step_no(b, layer, c) + 1)
                v.tensor_tensor(qs[32:C, par, :], post[0:32, :], row_coarse[:, :],
                                ALU.subtract).then_inc(row_split, 1)

            def norm(b, layer, c, k):
                n, hi = (32, 96) if layer == 0 else (C, P)
                at = step_no(b, layer, c) * 3
                if k == 0:
                    dve.wait_ge(sums_copied, step_no(b, layer, c) + 2)
                    v.transpose(inv_t[0:n, :], sums[0:n, :]).then_inc(norm_step, 1)
                if k == 1:
                    dve.wait_ge(norm_step, at + 1)
                    v.reciprocal(inv_c[C:hi, :], inv_t[0:n, 0:CHUNK:32]).then_inc(norm_step, 1)
                if k == 2:
                    dve.wait_ge(norm_step, at + 2)
                    v.transpose(inv[C:hi, :].rearrange("p (a b) -> p a b", b=32),
                                inv_c[C:hi, :].unsqueeze(2).to_broadcast([n, CHUNK // 32, 32])).then_inc(norm_step, 1)
                if k == 3:
                    dve.wait_ge(norm_step, at + 3)
                    o = (x_in if layer == 0 else pc)[C:hi, chunk(c)]
                    v.tensor_tensor(o, sums[C:hi, :], inv[C:hi, :], ALU.mult).then_inc(u_ready, 1)

            def split_post(b, layer, c):
                dve.wait_ge(post_coarse, step_no(b, layer, c) + 1)
                o = image_rows(y_pad, c)
                i, g = (a.rearrange("p (r w) -> p r w", w=W) for a in (post[:, :], coarse[:, 0, :]))
                if layer == 0:
                    v.tensor_tensor(o, i, g, ALU.subtract).then_inc(post_split, 1)
                else:
                    v.scalar_tensor_tensor(out=o, in0=i, scalar=bv_g[:, 0:1], in1=g, op0=ALU.add,
                                           op1=ALU.subtract).then_inc(post_split, 1)

            def attend(b, layer, c, par, first, last):
                end = last_units(layer)
                norm_at = ((0, 1, 1, 2), (1, 3, 5, 6))[layer]
                post_at = (3, 10)[layer]
                for t in range(TILES[layer]):
                    if not last:
                        for u in units_at(layer, t):
                            n = TILES[layer] // QT
                            take_max(b, layer, c + 1, 1 - par, u, u // n, u % n)
                        if t == end:
                            finish_max(b, layer, c + 1, 1 - par)
                    if not first:
                        for k in range(4):
                            if t == norm_at[k]:
                                norm(b, layer, c - 1, k)
                        if t == post_at:
                            split_post(b, layer, c - 1)
                if not last:
                    split_row(b, layer, c + 1, 1 - par)

            def branch(b, c, par, first, last):
                dve.wait_ge(part_ready, b * NCH + (c + 1))
                dve.wait_ge(feat_ready, b * NCH + (c + 1))
                v.tensor_tensor(bsum[0:C, par, :], work[0:C, par, :], part[0:C, par, :], ALU.add)
                v.tensor_tensor(bsum[C:P, par, :], work[C:P, 2 + par, :], part[C:P, par, :],
                                ALU.add).then_inc(branch_sum, 1)
                if first:
                    split_post(b, 1, NCH - 1)
                else:
                    stage_out(b, c - 1, 1 - par, first, last)

            def stage_out(b, c, par, first=False, last=False):
                dve.wait_ge(out_ready, b * NCH + (c + 1 + 2))
                dve.wait_ge(out_stored[par], b * (8 * NCH) + (c * 8 + (8 if par else 16)) )
                v.tensor_scalar(ostage[:, par, :], smax[0:C, par, :], col[0:C, B_OUT:B_OUT + 1], None,
                                ALU.add).then_inc(out_staged, 1)

            with dve.Fori(0, B) as b:
                for c in range(NCH):
                    dve.wait_ge(in0_ready, b * NCH + c + 1)
                    v.tensor_reduce(pooled[C:P, c * P:(c + 1) * P].rearrange("p (a k) -> p a k", a=ROWS // 2),
                                    work[C:P, c % 2, :].rearrange("p (a r k q) -> p a k r q", a=ROWS // 2, r=2, q=2),
                                    AX.XY, ALU.max).then_inc(pool_done, 1)
                    dve.wait_ge(theta_coarse, b * NCH + c + 1)
                    v.tensor_tensor(qall[:, chunk(c)].bitcast(F32R), work[0:32, c % 2, :], coarse[0:32, c % 2, :],
                                    ALU.subtract).then_inc(in0_used, 1)
                    dve.wait_ge(phi_coarse, b * NCH + c + 1)
                    v.tensor_tensor(keys[0:32, c * P:(c + 1) * P], pooled[C:96, c * P:(c + 1) * P],
                                    part[C:96, c % 2, 0:P], ALU.subtract).then_inc(phi_split, 1)
                for u in range(TILES[0]):
                    take_max(b, 0, 0, 0, u, u % QT, u // QT)
                finish_max(b, 0, 0, 0)
                dve.wait_ge(gt_ready, b + 1)
                v.tensor_copy(gt[:, :, C:96], wsum[:, 0:TILES[0] * 32].rearrange("p (t c) -> p t c", c=32))\
                    .then_inc(gt_copied, 1)
                split_row(b, 0, 0, 0)
                chunk_loop(dve, lambda c, par, first, last: attend(b, 0, c, par, first, last))
                for k in range(4):
                    norm(b, 0, NCH - 1, k)
                split_post(b, 0, NCH - 1)

                def qk_out(c):
                    dve.wait_ge(qk_coarse, b * NCH + c + 1)
                    for o, r in ((qall[:, chunk(c)].bitcast(F32R), slice(0, 32)), (keys[0:32, chunk(c)], slice(32, C))):
                        last = v.scalar_tensor_tensor(out=o, in0=work[r, 2 + c % 2, :], scalar=col[r, B_QK:B_QK + 1],
                                                      in1=coarse[r, c % 2, :], op0=ALU.add, op1=ALU.subtract)
                    last.then_inc(qk_split, 1)

                def cam_softmax():
                    e = post[0:C, 0:C]
                    dve.wait_ge(energy_ready, b + 1)
                    v.tensor_reduce(st[:, 0:1], e, AX.X, ALU.max).then_inc(cam_step, 1)
                    dve.wait_ge(cam_step, b * 5 + 1)
                    v.tensor_scalar(en[:, :], e, st[:, 0:1], -1.0, ALU.subtract, ALU.mult).then_inc(cam_step, 1)
                    dve.wait_ge(cam_step, b * 5 + 2)
                    v.tensor_reduce(st[:, 1:2], en[:, :], AX.X, ALU.max).then_inc(cam_step, 1)
                    dve.wait_ge(cam_step, b * 5 + 3)
                    v.tensor_scalar(st[:, 2:3], st[:, 1:2], -1.0, None, ALU.mult).then_inc(cam_step, 1)
                    dve.wait_ge(cam_exp, b + 1)
                    v.reciprocal(st[:, 4:5], st[:, 3:4]).then_inc(cam_step, 1)
                    dve.wait_ge(cam_step, b * 5 + 5)
                    for k in range(2):
                        last = v.tensor_scalar(attn[:, k, :], ex[:, :], st[:, 4:5],
                                               col[0:C, GAMMA_CA:GAMMA_CA + 1], ALU.mult, ALU.mult)
                    last.then_inc(attn_ready, 1)

                for c in range(2, NCH + 3):
                    if c - 2 < NCH:
                        dve.wait_ge(tr_ready, b * NCH + c - 1)
                        v.tensor_copy(pt_ct[:, QT * (c - 2):QT * (c - 1), C:3 * C],
                                      wsum[:, :].rearrange("p (t c) -> p t c", t=QT)).then_inc(tr_copied, 1)
                        qk_out(c - 2)
                    if c >= 3:
                        for lt in range(QT):
                            take_max(b, 1, 0, 0, (c - 3) * QT + lt, lt, c - 3)
                finish_max(b, 1, 0, 0)
                cam_softmax()
                dve.wait_ge(attn_t_ready, b + 1)
                v.tensor_tensor(cam_w[C:P, :], wsum[C:P, 0:P], two_idn[C:P, :], ALU.add).then_inc(cam_w_ready, 1)
                split_row(b, 1, 0, 0)
                for c in range(NCH):
                    dve.wait_ge(cam_coarse, b * NCH + c + 1)
                    v.tensor_tensor(image_rows(c_pad, c), work[:, c % 2, :].rearrange("p (r w) -> p r w", w=W),
                                    coarse[:, c % 2, :].rearrange("p (r w) -> p r w", w=W),
                                    ALU.subtract).then_inc(cam_split, 1)
                chunk_loop(dve, lambda c, par, first, last: attend(b, 1, c, par, first, last))
                for k in range(4):
                    norm(b, 1, NCH - 1, k)
                chunk_loop(dve, lambda c, par, first, last: branch(b, c, par, first, last))
                stage_out(b, NCH - 1, 1)


N_LOADS = 18


def kernel(**inputs):
    import numpy as np
    import concourse.bacc as bacc
    from concourse.bass_utils import run_bass_kernel_spmd

    g = {k: np.ascontiguousarray(v) for k, v in inputs.items()}
    f = np.float32

    def l1(name):
        return g["L1_conv_" + name]

    zero = np.zeros((C, 32), f)
    w_in0 = np.concatenate([np.tile(g["L0_conv_w_theta"].T, (1, 4)), zero, np.tile(g["L0_conv_w_phi"].T, (1, 4)),
                            g["L0_conv_w_g"].T], axis=1)
    w_o0 = np.tile(g["L0_conv_w_o"].T, (1, 2))
    w_qk = np.concatenate([np.tile(l1("wq").T, (1, 4)), np.tile(l1("wk").T, (1, 4))], axis=1)
    w_v = np.tile(l1("wv").T, (1, 2))

    def taps(w):
        return w.transpose(1, 2, 3, 0).reshape(C, TAPS, C)

    w_c1 = np.tile(np.concatenate([taps(l1("w_pam1")), taps(l1("w_cam1"))], axis=2), (2, 1, 1)).reshape(P, TAPS * P)
    w_c2p = np.tile(taps(l1("w_pam2")), (2, 1, 1)).reshape(P, TAPS * C)
    w_c2c = np.tile(taps(l1("w_cam2")), (2, 1, 1)).reshape(P, TAPS * C)
    w_out = np.tile(l1("w_out").T, (2, 1))
    cols = np.zeros((P, NCOL), f)
    for k, n in ((0, "1"), (4, "2")):
        for i, s in enumerate("gbmv"):
            cols[:, k + i] = np.concatenate([l1(f"bn_pam{n}_{s}"), l1(f"bn_cam{n}_{s}")])
    cols[:C, B_QK] = np.concatenate([np.tile(l1("bq"), 4), np.tile(l1("bk"), 4)])
    cols[:, B_V] = np.tile(l1("bv"), 2)
    cols[:C, B_OUT] = l1("b_out")
    cols[:, GAMMA0] = g["L0_conv_gamma"]
    cols[:, GAMMA_PA] = l1("gamma_pa")
    cols[:, GAMMA_CA] = l1("gamma_ca")
    cols[C:, MASK_HALF] = 1
    group = np.arange(32) // C8
    cols[:32, MASK_QK] = group // 2
    cols[32:64, MASK_QK] = group % 2
    cols[64:96, MASK_QK] = group % 2
    cols[1, MASK_ROW] = 1
    arrays = {"x": g["x"].reshape(B, C, L), "cols": cols, "ident": np.eye(P, dtype=f), "w_in0": w_in0, "w_o0": w_o0,
              "w_qk": w_qk, "w_v": w_v, "w_c1": w_c1, "w_c2p": w_c2p, "w_c2c": w_c2c, "w_out": w_out}
    arrays = {f"in_{k}": np.ascontiguousarray(a) for k, a in arrays.items()}
    nc = bacc.Bacc("TRN2", target_bir_lowering=False, num_devices=1)
    args = [nc.dram_tensor(k, a.shape, mybir.dt.from_np(a.dtype), kind="ExternalInput").ap() for k, a in arrays.items()]
    args.append(nc.dram_tensor("out_0", (B, C, L), F32, kind="ExternalOutput").ap())
    build(nc, *args)
    r = run_bass_kernel_spmd(nc, [arrays], core_ids=[0])
    return r.results[0]["out_0"].reshape(B, C, H, W)
```

```python
from contextlib import ExitStack

import concourse.bass as bass
from concourse import mybir

ALU = mybir.AluOpType
ACT = mybir.ActivationFunctionType
AX = mybir.AxisListType
F32 = mybir.dt.float32
F32R = mybir.dt.float32r

B, C, H, W = 16, 64, 64, 64
L = H * W
P = 128
CHUNK = 512
NCH = L // CHUNK
ROWS = CHUNK // W
QT = CHUNK // P
HP, WP = H + 2, W + 2
TAPS = 9
C8, C2 = C // 8, C // 2
KEYS = (L // 4, L)
TILES = (KEYS[0] // P, KEYS[1] // P)
TILE_OFF = (0, TILES[0] * NCH)
GROUP = 4
GROUPS = TILES[1] // GROUP
PAIRS = (TILES[0] // 2, TILES[1] // 2)
PAIRS_ALL = (PAIRS[0] + PAIRS[1]) * NCH
TILES_ALL = (TILES[0] + TILES[1]) * NCH
STEPS = 2 * NCH
UNITS = (4, 5, 5, 5, 4, 5, 4, 0)
FIRST_UNIT = tuple(sum(UNITS[:g]) for g in range(GROUPS + 1))
POST_GROUP = 4
POST_UNIT = FIRST_UNIT[POST_GROUP] + 1
assert POST_UNIT % 2 == 0
(BN1_G, BN1_B, BN1_M, BN1_V, BN2_G, BN2_B, BN2_M, BN2_V, B_QK, B_V, B_OUT, GAMMA0, GAMMA_PA, GAMMA_CA,
 MASK_HALF, MASK_QK) = range(16)
NCOL = 16


def build(nc, x, cols, ident, w_in0, w_o0, w_qk, w_v, w_c1, w_c2p, w_c2c, w_out, out):
    ctx = ExitStack()
    with ctx:
        def sb(name, shape, dt=F32):
            return ctx.enter_context(nc.sbuf_tensor(name, shape, dt))

        def sem(name):
            return ctx.enter_context(nc.semaphore(name))

        work = ctx.enter_context(nc.psum_tensor("work", [P, 4, CHUNK], F32))
        ring = ctx.enter_context(nc.psum_tensor("ring", [P, 2, CHUNK], F32))
        acc = ctx.enter_context(nc.psum_tensor("acc", [P, 2, CHUNK], F32))

        col = sb("col", [P, NCOL])
        idn = sb("idn", [P, P])
        neg_idn = sb("neg_idn", [P, P])
        two_idn = sb("two_idn", [P, P])
        wi0 = sb("wi0", [P, P])
        proj_y = sb("proj_y", [P, P])
        proj_p = sb("proj_p", [P, P])
        wqk = sb("wqk", [P, C])
        w1 = sb("w1", [P, 2, TAPS, P], F32R)
        w2p = sb("w2p", [P, TAPS, P], F32R)
        w2c = sb("w2c", [P, TAPS, P], F32R)
        wout = sb("wout", [P, C])
        bn = sb("bn", [P, 2, 6])
        bqk_m = sb("bqk_m", [C, 1])
        bv_g = sb("bv_g", [P, 2])

        x_in = sb("x_in", [P, L])
        y_pad = sb("y_pad", [P, HP, WP], F32R)
        c_pad = sb("c_pad", [P, HP, WP], F32R)
        pc = sb("pc", [P, L])
        pt_ct = sb("pt_ct", [P, TILES[1], 2 * C])
        gt = sb("gt", [P, TILES[0], 2 * C2])
        ones = sb("ones", [P, C])
        keys = sb("keys", [P, L], F32R)
        qall = sb("qall", [C, L])
        qs = sb("qs", [P, 2, CHUNK], F32R)
        pooled = sb("pooled", [P, KEYS[0]])
        probs = sb("probs", [P, 2 * GROUP, CHUNK])
        duos = sb("duos", [P, 2, CHUNK])
        quads = sb("quads", [P, 4, CHUNK])
        upper_lower = sb("upper_lower", [P, 2, CHUNK])
        half_num = upper_lower[0:C, 0, :]
        inv_t = upper_lower[0:C, 1, :]
        ostage = upper_lower[C:P, :, :]
        half_sum = sb("half_sum", [C, CHUNK])
        sums = sb("sums", [C, CHUNK])
        wnum = sb("wnum", [P, CHUNK])
        inv_c = sb("inv_c", [P, CHUNK // 32])
        inv = sb("inv", [P, CHUNK])
        mx = sb("mx", [P, 2, QT, 8])
        mx1 = sb("mx1", [P, 2, QT])
        mx_cols = sb("mx_cols", [P, 2, QT, 32])
        coarse = sb("coarse", [P, 2, CHUNK])
        part = sb("part", [P, 2, CHUNK])
        bsum = sb("bsum", [P, 2, CHUNK])
        feat = sb("feat", [P, 2, CHUNK])
        en = sb("en", [C, C])
        ex = sb("ex", [C, C])
        attn = sb("attn", [C, 2, C])
        cam_w = sb("cam_w", [P, P])
        st = sb("st", [C, 6])
        wtmp = pc

        consts_in = sem("consts_in")
        consts_ready = sem("consts_ready")
        setup_act = sem("setup_act")
        setup_dve = sem("setup_dve")
        x_loaded = sem("x_loaded")
        in0_ready = sem("in0_ready")
        theta_coarse = sem("theta_coarse")
        in0_used = sem("in0_used")
        phi_coarse = sem("phi_coarse")
        pool_done = sem("pool_done")
        phi_split = sem("phi_split")
        gt_ready = sem("gt_ready")
        gt_copied = sem("gt_copied")
        staged = sem("staged")
        smax_ready = sem("smax_ready")
        max_done = sem("max_done")
        mx_step = sem("mx_step")
        mx_ready = sem("mx_ready")
        row_ready = sem("row_ready")
        row_in = sem("row_in")
        scores_ready = sem("scores_ready")
        exp_done = sem("exp_done")
        probs_used = sem("probs_used")
        duo_ready = sem("duo_ready")
        quad_ready = sem("quad_ready")
        ones_done = sem("ones_done")
        num_half = sem("num_half")
        sum_half = sem("sum_half")
        num_taken = sem("num_taken")
        sum_taken = sem("sum_taken")
        norm_step = sem("norm_step")
        u_ready = sem("u_ready")
        post_ready = sem("post_ready")
        post_coarse = sem("post_coarse")
        post_split = sem("post_split")
        conv1_ready = sem("conv1_ready")
        pc_ready = sem("pc_ready")
        tr_ready = sem("tr_ready")
        tr_copied = sem("tr_copied")
        energy_ready = sem("energy_ready")
        cam_step = sem("cam_step")
        cam_exp = sem("cam_exp")
        attn_ready = sem("attn_ready")
        attn_t_ready = sem("attn_t_ready")
        cam_w_ready = sem("cam_w_ready")
        qk_ready = sem("qk_ready")
        qk_coarse = sem("qk_coarse")
        qk_split = sem("qk_split")
        cam_ready = sem("cam_ready")
        cam_coarse = sem("cam_coarse")
        cam_split = sem("cam_split")
        conv2_ready = sem("conv2_ready")
        part_ready = sem("part_ready")
        branch_sum = sem("branch_sum")
        feat_ready = sem("feat_ready")
        out_ready = sem("out_ready")
        out_staged = sem("out_staged")
        out_stored = [sem(f"out_stored{i}") for i in range(2)]

        def tile_no(b, layer, c, u):
            return b * TILES_ALL + c * TILES[layer] + (layer * NCH * TILES[0] + u)

        def pair_no(b, layer, c, q):
            return b * PAIRS_ALL + c * PAIRS[layer] + (layer * NCH * PAIRS[0] + q)

        def step_no(b, layer, c):
            return b * STEPS + (c + NCH * layer)

        def chunk(c):
            return bass.ds(c * CHUNK, CHUNK)

        def image_rows(tile, c):
            return tile[:, bass.ds(c * ROWS + 1, ROWS), 1:1 + W]

        def chunk_loop(eng, step, before, after):
            for c in range(before):
                step(c, c % 2)
            with eng.Fori(0, (NCH - before - after) // 2) as turn:
                for k in range(2):
                    step(turn * 2 + (before + k), (before + k) % 2)
            for c in range(NCH - after, NCH):
                step(c, c % 2)

        def post_out(layer, c, odd):
            if layer == 0:
                return acc[:, 1 - odd, :]
            return ring[:, int(is_last(c)), :]

        def early(c, n):
            return isinstance(c, int) and c < n

        def is_last(c):
            return isinstance(c, int) and c == NCH - 1

        def settle(eng):
            eng.wait_ge(consts_ready, 1)

        block = ctx.enter_context(nc.Block())

        @block.sync
        def _(sp):
            loads = [(col[:], cols), (idn[:], ident), (two_idn[0:C, 0:C], ident[0:C, 0:C]),
                     (two_idn[0:C, C:P], ident[0:C, 0:C]), (two_idn[C:P, 0:C], ident[0:C, 0:C]),
                     (two_idn[C:P, C:P], ident[0:C, 0:C]), (wi0[0:C, :], w_in0), (proj_y[C:96, :], w_o0),
                     (proj_p[C:P, :], w_v), (wqk[0:C, :], w_qk), (wtmp[:, 0:TAPS * P], w_c1),
                     (wtmp[:, TAPS * P:TAPS * (P + C)], w_c2p), (wtmp[:, TAPS * (P + C):TAPS * 2 * P], w_c2c),
                     (wout[:], w_out), (proj_y[0:C, 0:C], ident[0:C, 0:C]), (proj_y[0:C, C:P], ident[0:C, 0:C]),
                     (proj_p[0:C, 0:C], ident[0:C, 0:C]), (proj_p[0:C, C:P], ident[0:C, 0:C])]
            assert len(loads) == N_LOADS
            for dst, src in loads:
                sp.dma_start(dst, src).then_inc(consts_in, 16)
            for s in out_stored:
                sp.sem_inc(s, 16)
            sp.dma_start(x_in[0:C, :], x[0]).then_inc(x_loaded, 16)

            def store(b, c, par):
                sp.wait_ge(out_staged, b * NCH + (c + 1 + 2))
                sp.dma_start(out_view(b, c), ostage[:, par, :]).then_inc(out_stored[par], 16)

            def out_view(b, c):
                return out[bass.ds(b, 1), :, chunk(c)].rearrange("o c l -> (o c) l")

            def stores(b):
                chunk_loop(sp, lambda c, par: store(b, c, par), 0, 0)

            with sp.Fori(0, B - 1) as b:
                sp.wait_ge(post_ready, b * STEPS + NCH)
                sp.dma_start(x_in[0:C, :], x[bass.ds(b + 1, 1)].rearrange("o c l -> (o c) l")).then_inc(x_loaded, 16)
                stores(b)
            sp.wait_ge(post_ready, (B - 1) * STEPS + NCH)
            sp.dma_start(x_in[0:C, :], x[B - 1]).then_inc(x_loaded, 16)
            stores(B - 1)
            for s in out_stored:
                sp.wait_ge(s, 16 + B * NCH // 2 * 16)

        @block.gpsimd
        def _(pool):
            pool.sem_inc(quad_ready, 2)

            def quad(b, c, g):
                at = b * (NCH * GROUPS) + (c * GROUPS + g)
                slot = GROUP * (g % 2)
                pool.wait_ge(exp_done, pair_no(b, 1, c, 2 * g + 2 + 2))
                pool.wait_ge(quad_ready, at + 2)
                nc.gpsimd.tensor_tensor(duos[:, :, :], probs[:, slot:slot + 2, :], probs[:, slot + 2:slot + 4, :],
                                        ALU.add).then_inc(duo_ready, 1)
                if g % 2 == 0:
                    pool.wait_ge(ones_done, b * (NCH * GROUPS // 2) + (c * (GROUPS // 2) + g // 2 + 1))
                pool.wait_ge(duo_ready, at + 1)
                nc.gpsimd.tensor_tensor(quads[:, g % 4, :], duos[:, 0, :], duos[:, 1, :],
                                        ALU.add).then_inc(quad_ready, 1)

            def divide(b, c):
                pool.wait_ge(norm_step, step_no(b, 0, c) * 3 + 3)
                nc.gpsimd.tensor_tensor(x_in[C:96, chunk(c)], sums[C2:C, :], inv[C2:C, :], ALU.mult)\
                    .then_inc(u_ready, 1)

            with pool.Fori(0, B) as b:
                with pool.Fori(0, NCH) as c:
                    divide(b, c)
                with pool.Fori(0, NCH) as c:
                    for g in range(GROUPS):
                        quad(b, c, g)

        @block.tensor
        def _(pe):
            def mm(o, a, r, start=True, stop=True):
                return nc.tensor.matmul(o, a, r, start=start, stop=stop)

            pe.sem_inc(probs_used, 4)
            pe.sem_inc(ones_done, 2)
            pe.sem_inc(out_ready, 2)
            pe.wait_ge(consts_ready, 1)

            def max_unit(b, layer, c, par, u, bank, before=None):
                n = TILES[layer] // QT
                lt, kc = u if isinstance(u, tuple) else (u // n, u % n)
                if before is not None:
                    pe.wait_ge(max_done, tile_no(b, layer, c, before + 1 + 2))
                mm(ring[:, bank, :], qs[:, par, lt * P:(lt + 1) * P],
                   keys[:, kc * CHUNK:(kc + 1) * CHUNK]).then_inc(smax_ready, 1)

            def max_row(b, layer, c, par, bank):
                pe.wait_ge(mx_ready, step_no(b, layer, c) + 1)
                for lt in range(QT):
                    last = mm(ring[0:32, bank, lt * P:(lt + 1) * P], mx_cols[:, par, lt, :], neg_idn[:, :])
                last.then_inc(row_ready, 1)

            def project(b, layer, c, odd):
                pe.wait_ge(u_ready, step_no(b, layer, c) + 1 + 1)
                w, r = (proj_y, x_in) if layer == 0 else (proj_p, pc)
                mm(post_out(layer, c, odd), w[:, :], r[:, chunk(c)]).then_inc(post_ready, 1)

            def score_pair(b, layer, c, par, q):
                pe.wait_ge(exp_done, pair_no(b, layer, c, q + 1))
                for t in (2 * q, 2 * q + 1):
                    last = mm(work[:, t % 4, :], keys[:, t * P:(t + 1) * P], qs[:, par, :])
                last.then_inc(scores_ready, 1)

            def weigh_pair(b, layer, c, par, q):
                pe.wait_ge(exp_done, pair_no(b, layer, c, q + 1 + 2))
                if q == 0 and layer == 0:
                    pe.wait_ge(sum_taken, step_no(b, 0, c) + 1)
                    if not early(c, 2):
                        pe.wait_ge(post_split, step_no(b, 0, c) - 2 + 1)
                if q == 0 and layer == 1:
                    pe.wait_ge(num_taken, b * NCH + (c + 1))
                for t in (2 * q, 2 * q + 1):
                    h = C * (t % 2)
                    w, bank = (gt[:, t, :], par) if layer == 0 else (pt_ct[:, t, 0:C], 0)
                    last = mm(acc[h:h + C, bank, :], w, probs[:, t % 8, :], start=(q == 0),
                              stop=(q == PAIRS[layer] - 1))
                last.then_inc(probs_used, 1)

            def sum_pair(b, c, k):
                pe.wait_ge(quad_ready, b * (NCH * GROUPS) + (c * GROUPS + 2 * k + 2 + 2))
                if k == 0:
                    pe.wait_ge(sum_taken, step_no(b, 1, c) + 2)
                for h in range(2):
                    last = mm(acc[C * h:C * h + C, 1, :], ones[:, :], quads[:, (2 * k + h) % 4, :], start=(k == 0),
                              stop=(k == GROUPS // 2 - 1))
                last.then_inc(ones_done, 1)

            def attend0(b, c, par):
                nxt = not is_last(c)

                def unit(u):
                    if nxt:
                        max_unit(b, 0, c + 1, 1 - par, u, u % 2, u - 2 if u >= 2 else None)
                if nxt:
                    pe.wait_ge(staged, step_no(b, 0, c) + 2)
                unit(0)
                pe.wait_ge(row_in, step_no(b, 0, c) + 1)
                score_pair(b, 0, c, par, 0)
                unit(1)
                score_pair(b, 0, c, par, 1)
                unit(2)
                weigh_pair(b, 0, c, par, 0)
                unit(3)
                score_pair(b, 0, c, par, 2)
                unit(4)
                weigh_pair(b, 0, c, par, 1)
                unit(5)
                score_pair(b, 0, c, par, 3)
                unit(6)
                if not early(c, 2):
                    pe.wait_ge(sum_taken, step_no(b, 0, c) + 2)
                    project(b, 0, c - 2, par)
                unit(7)
                weigh_pair(b, 0, c, par, 2)
                if nxt:
                    max_row(b, 0, c + 1, 1 - par, 1)
                weigh_pair(b, 0, c, par, 3)

            def attend1(b, c, par):
                nxt, before = not is_last(c), not early(c, 1)
                late = POST_UNIT
                if nxt:
                    pe.wait_ge(staged, step_no(b, 1, c) + 2)
                for g in range(GROUPS):
                    units = list(range(FIRST_UNIT[g], FIRST_UNIT[g + 1])) if nxt else []

                    def unit():
                        if units:
                            u = units.pop(0)
                            if before and u == late + 1:
                                pe.wait_ge(post_split, step_no(b, 1, c) + 1)
                            max_unit(b, 1, c + 1, 1 - par, u, (u + (u >= late)) % 2,
                                     u - 1 if u == late else u - 2 if u >= 2 else None)
                    post = g == POST_GROUP and before
                    if g == 0:
                        unit()
                        pe.wait_ge(row_in, step_no(b, 1, c) + 1)
                    score_pair(b, 1, c, par, 2 * g)
                    unit()
                    if post:
                        if nxt:
                            pe.wait_ge(max_done, tile_no(b, 1, c + 1, late - 2 + 1 + 2))
                        project(b, 1, c - 1, 1 - par)
                        unit()
                    if g == 0 and before:
                        weigh_pair(b, 1, c - 1, 1 - par, 2 * GROUPS - 1)
                        unit()
                    score_pair(b, 1, c, par, 2 * g + 1)
                    if not post:
                        unit()
                    if g >= 1:
                        weigh_pair(b, 1, c, par, 2 * g - 2)
                    if g == GROUPS - 1 and nxt:
                        max_row(b, 1, c + 1, 1 - par, 1)
                    while len(units) > 1 and not post:
                        unit()
                    if g >= 1:
                        weigh_pair(b, 1, c, par, 2 * g - 1)
                    while units:
                        unit()
                    if g == 1 and before:
                        sum_pair(b, c - 1, GROUPS // 2 - 1)
                    if g % 2 == 1 and g >= 3:
                        sum_pair(b, c, (g - 3) // 2)
                weigh_pair(b, 1, c, par, 2 * GROUPS - 2)

            def proj0(b, c, par):
                if early(c, 1):
                    pe.wait_ge(x_loaded, b * 16 + 16)
                    pe.wait_ge(num_taken, b * NCH + 1)
                elif early(c, 2):
                    pe.wait_ge(sum_taken, step_no(b, 0, 0) + 2)
                else:
                    pe.wait_ge(in0_used, b * NCH + (c - 1))
                mm(acc[:, par, :], wi0[:, :], x_in[:, chunk(c)]).then_inc(in0_ready, 1)

            def conv1(b, c, between=()):
                if c == 0:
                    pe.wait_ge(post_split, step_no(b, 0, NCH - 2) + 1)
                if c == 5:
                    pe.wait_ge(post_split, step_no(b, 0, NCH) + 1)
                if c >= 2:
                    pe.wait_ge(pc_ready, b * NCH + (c - 1))
                between = list(between)
                for i in range(2 * TAPS):
                    half, tap = divmod(i, TAPS)
                    dy, dx = divmod(tap, 3)
                    last = mm(work[:, c % 2, :], w1[:, half, tap, :],
                              y_pad[:, ROWS * c + dy:ROWS * c + dy + ROWS, dx:dx + W],
                              start=(i == 0), stop=(i == 2 * TAPS - 1))
                    if i == 2 * TAPS - 1:
                        last.then_inc(conv1_ready, 1)
                    if i % 3 == 1 and i >= TAPS - 2 and between:
                        between.pop(0)()

            def transposes(b, c):
                if c == 0:
                    pe.wait_ge(post_split, step_no(b, 0, NCH - 1) + 1)
                if c >= 1:
                    pe.wait_ge(tr_copied, b * NCH + c)
                for i in range(QT):
                    t = QT * c + i
                    last = nc.tensor.transpose(acc[:, 1, i * P:(i + 1) * P], pc[:, t * P:(t + 1) * P], idn[:, :])
                last.then_inc(tr_ready, 1)

            def energy(b, c):
                if c == 0:
                    pe.wait_ge(post_split, step_no(b, 0, NCH) + 1)
                pe.wait_ge(tr_copied, b * NCH + c + 1)
                for i in range(QT):
                    t = QT * c + i
                    ct = pt_ct[:, t, C:2 * C]
                    last = mm(acc[0:C, 0, 0:C], ct, ct, start=(t == 0), stop=(t == TILES[1] - 1))
                if c == NCH - 1:
                    last.then_inc(energy_ready, 1)

            def query_key(b, c):
                pe.wait_ge(pc_ready, b * NCH + c + 1)
                if c >= 2:
                    pe.wait_ge(qk_split, b * NCH + (c - 1))
                mm(work[0:C, 2 + c % 2, :], wqk[:, :], pc[:, chunk(c)]).then_inc(qk_ready, 1)

            def conv2(b, c, par):
                if early(c, 1):
                    pe.wait_ge(post_split, step_no(b, 1, NCH - 1) + 1)
                pe.wait_ge(branch_sum, b * NCH + (c + 1))
                for k, (pad, w) in enumerate(((y_pad, w2p), (c_pad, w2c))):
                    for tap in range(TAPS):
                        dy, dx = divmod(tap, 3)
                        end = mm(work[:, 2 * k + par, :], w[:, tap, :],
                                 pad[:, bass.ds(c * ROWS + dy, ROWS), dx:dx + W],
                                 start=(tap == 0), stop=(tap == TAPS - 1))
                end.then_inc(conv2_ready, 1)
                proj0(b + 1, c, par)
                if early(c, 1):
                    sum_pair(b, NCH - 1, GROUPS // 2 - 1)
                else:
                    if early(c, 2):
                        project(b, 1, NCH - 1, 1)
                    out_project(b, c - 1, 1 - par)
                    if early(c, 2):
                        settle(pe)
                        pe.wait_ge(post_split, step_no(b, 1, NCH) + 1)

            def out_project(b, c, par):
                pe.wait_ge(feat_ready, b * NCH + (c + 1 + 2))
                pe.wait_ge(out_staged, b * NCH + (c + 1))
                mm(ring[0:C, par, :], wout[:, :], feat[:, par, :]).then_inc(out_ready, 1)

            chunk_loop(pe, lambda c, par: proj0(0, c, par), 2, 0)
            with pe.Fori(0, B) as b:
                pe.wait_ge(out_staged, b * NCH + 2)
                pe.wait_ge(phi_split, b * NCH + NCH)
                pe.wait_ge(staged, step_no(b, 0, 0) + 1)
                for u in range(TILES[0]):
                    max_unit(b, 0, 0, 0, (u % QT, u // QT), u % 2, u - 2 if u >= 2 else None)
                settle(pe)
                pe.wait_ge(pool_done, b * NCH + NCH)
                for t in range(TILES[0]):
                    last = nc.tensor.transpose(acc[:, 0, t * 32:(t + 1) * 32], pooled[96:P, t * P:(t + 1) * P],
                                               idn[96:P, 96:P])
                last.then_inc(gt_ready, 1)
                max_row(b, 0, 0, 0, 1)
                pe.wait_ge(gt_copied, b + 1)
                chunk_loop(pe, lambda c, par: attend0(b, c, par), 2, 2)

                conv1(b, 0)
                pe.wait_ge(sum_taken, step_no(b, 0, NCH) + 2)
                project(b, 0, NCH - 2, 0)

                def first_unit(kc, lt):
                    u = kc * QT + lt
                    if u == 0:
                        pe.wait_ge(staged, step_no(b, 1, 0) + 1)
                    if lt == 0:
                        pe.wait_ge(qk_split, b * NCH + (kc + 1))
                    max_unit(b, 1, 0, 0, (lt, kc), u % 2, u - 2 if u >= 2 else None)
                for c in range(1, NCH + 2):
                    units = [lambda kc=c - 2, lt=lt: first_unit(kc, lt) for lt in range(QT)] if c >= 2 else []
                    if c < NCH:
                        conv1(b, c, units)
                        units = []
                    if c >= 2:
                        energy(b, c - 2)
                    for unit in units[:2] if c == NCH else []:
                        unit()
                    if c - 1 < NCH:
                        query_key(b, c - 1)
                        transposes(b, c - 1)
                    for unit in units[2:] if c == NCH else units:
                        unit()
                    if c == 1:
                        project(b, 0, NCH - 1, 1)
                max_row(b, 1, 0, 0, 1)
                pe.wait_ge(attn_ready, b + 1)
                mm(acc[:, 1, 0:P], attn[:, :, :].rearrange("c a d -> c (a d)"), two_idn[0:C, :])\
                    .then_inc(attn_t_ready, 1)
                pe.wait_ge(cam_w_ready, b + 1)
                for c in range(NCH):
                    if c >= 4:
                        pe.wait_ge(cam_split, b * NCH + (c - 3))
                    mm(work[:, c % 4, :], cam_w[:, :], pc[:, chunk(c)]).then_inc(cam_ready, 1)
                pe.wait_ge(cam_split, b * NCH + NCH)
                pe.wait_ge(cam_split, b * NCH + NCH)
                chunk_loop(pe, lambda c, par: attend1(b, c, par), 1, 1)
                weigh_pair(b, 1, NCH - 1, 1, 2 * GROUPS - 1)
                chunk_loop(pe, lambda c, par: conv2(b, c, par), 2, 0)
                out_project(b, NCH - 1, 1)

        @block.scalar
        def _(act):
            def affine(o, i, scale=1.0, bias=0.0):
                return nc.scalar.activation(o, i, ACT.Identity, bias=bias, scale=scale)

            act.sem_inc(exp_done, 2)
            act.sem_inc(feat_ready, 2)
            act.wait_ge(setup_dve, 1)
            for k in range(2):
                nc.scalar.activation(bn[:, k, 1:2], bn[:, k, 0:1], ACT.Sqrt).then_inc(setup_act, 1)
            act.wait_ge(consts_ready, 1)

            def stage(b, layer, c, par):
                nc.scalar.copy(qs[0:C, par, :], qall[:, chunk(c)]).then_inc(staged, 1)

            def copy_num(b, c):
                act.wait_ge(probs_used, pair_no(b, 1, c + 1, 4))
                act.wait_ge(num_taken, b * NCH + (c + 1))
                nc.scalar.copy(half_num[:, :], acc[C:P, 0, :]).then_inc(num_half, 1)

            def copy_sum(b, layer, c, par):
                if layer == 0:
                    act.wait_ge(probs_used, pair_no(b, 0, c + 1, 4))
                else:
                    act.wait_ge(ones_done, b * (NCH * GROUPS // 2) + (c * (GROUPS // 2) + (GROUPS // 2 + 2)))
                act.wait_ge(sum_taken, step_no(b, layer, c) + 2)
                nc.scalar.copy(half_sum[:, :], acc[C:P, par if layer == 0 else 1, :]).then_inc(sum_half, 1)

            def split_post(b, layer, c, odd):
                act.wait_ge(post_ready, step_no(b, layer, c) + 1)
                act.wait_ge(post_split, step_no(b, layer, c) + 1)
                affine(coarse[:, 0, :].bitcast(F32R), post_out(layer, c, odd), scale=col[:, MASK_HALF:MASK_HALF + 1],
                       bias=bv_g[:, 1:2] if layer else 0.0).then_inc(post_coarse, 1)

            def row(b, layer, c, par, bank):
                act.wait_ge(row_ready, step_no(b, layer, c) + 1)
                nc.scalar.copy(qs[32:C, par, :], ring[0:32, bank, :]).then_inc(row_in, 1)

            def exponentials(b, layer, c, q):
                act.wait_ge(scores_ready, pair_no(b, layer, c, q + 1))
                act.wait_ge(probs_used, pair_no(b, layer, c, q + 1))
                if layer == 1 and q % 2 == 0:
                    act.wait_ge(quad_ready, b * (NCH * GROUPS) + (c * GROUPS + q // 2 + 1))
                s = 2 * q
                nc.scalar.activation(probs[:, s % 8:s % 8 + 2, :], work[:, s % 4:s % 4 + 2, :],
                                     ACT.Exp).then_inc(exp_done, 1)

            def attend0(b, c, par):
                if not is_last(c):
                    stage(b, 0, c + 1, 1 - par)
                row(b, 0, c, par, 1)
                exponentials(b, 0, c, 0)
                if not early(c, 1):
                    copy_sum(b, 0, c - 1, 1 - par)
                exponentials(b, 0, c, 1)
                exponentials(b, 0, c, 2)
                exponentials(b, 0, c, 3)
                if not early(c, 2):
                    split_post(b, 0, c - 2, par)

            def attend1(b, c, par):
                before = not early(c, 1)
                if not is_last(c):
                    stage(b, 1, c + 1, 1 - par)
                if before:
                    row(b, 1, c, par, 1)
                for g in range(GROUPS):
                    exponentials(b, 1, c, 2 * g)
                    if before:
                        if g == 2:
                            copy_sum(b, 1, c - 1, 1 - par)
                        if g == POST_GROUP:
                            split_post(b, 1, c - 1, 1 - par)
                    exponentials(b, 1, c, 2 * g + 1)
                    if before and g == 0:
                        copy_num(b, c - 1)

            def in0(b, c, par):
                act.wait_ge(in0_ready, b * NCH + (c + 1))
                if not early(c, 2):
                    act.wait_ge(in0_used, b * NCH + (c - 1))
                    act.wait_ge(phi_split, b * NCH + (c - 1))
                    act.wait_ge(post_split, step_no(b, 0, 0) + 1)
                elif early(c, 1) and not isinstance(b, int):
                    act.wait_ge(post_split, step_no(b, 0, 0))
                affine(coarse[0:32, par, :].bitcast(F32R), acc[0:32, par, :],
                       scale=col[0:32, MASK_QK:MASK_QK + 1]).then_inc(theta_coarse, 1)
                act.wait_ge(pool_done, b * NCH + (c + 1))
                affine(coarse[C:96, par, 0:P].bitcast(F32R), pooled[C:96, bass.ds(c * P, P)],
                       scale=col[C:96, MASK_QK:MASK_QK + 1]).then_inc(phi_coarse, 1)

            def conv1_out(b, c):
                act.wait_ge(conv1_ready, b * NCH + c + 1)
                nc.scalar.activation(pc[:, chunk(c)], work[:, c % 2, :], ACT.Relu, bias=bn[:, 0, 5:6],
                                     scale=bn[:, 0, 4:5]).then_inc(pc_ready, 1)

            def qk_out(b, c):
                act.wait_ge(qk_ready, b * NCH + c + 1)
                if c >= 2:
                    act.wait_ge(qk_split, b * NCH + (c - 1))
                affine(coarse[0:C, c % 2, :].bitcast(F32R), work[0:C, 2 + c % 2, :],
                       scale=col[0:C, MASK_QK:MASK_QK + 1], bias=bqk_m[:, :]).then_inc(qk_coarse, 1)

            def conv2_out(b, c, par):
                if not early(c, 1):
                    features(b, c - 1, 1 - par)
                act.wait_ge(conv2_ready, b * NCH + (c + 1))
                act.wait_ge(branch_sum, b * NCH + (c + 1))
                nc.scalar.copy(part[0:C, par, :], work[C:P, par, :])
                nc.scalar.copy(part[C:P, par, :], work[0:C, 2 + par, :]).then_inc(part_ready, 1)
                if early(c, 1):
                    copy_sum(b, 1, NCH - 1, 1)
                elif early(c, 2):
                    act.wait_ge(phi_split, b * NCH + (NCH + 1))
                    split_post(b, 1, NCH - 1, 1)
                in0(b + 1, c, par)

            def features(b, c, par):
                act.wait_ge(branch_sum, b * NCH + (c + 1 + 2))
                act.wait_ge(out_ready, b * NCH + (c + 1))
                nc.scalar.activation(feat[:, par, :], bsum[:, par, :], ACT.Relu, bias=bn[:, 1, 5:6],
                                     scale=bn[:, 1, 4:5]).then_inc(feat_ready, 1)

            chunk_loop(act, lambda c, par: in0(0, c, par), 2, 0)
            with act.Fori(0, B) as b:
                act.wait_ge(in0_used, b * NCH + NCH)
                stage(b, 0, 0, 0)
                chunk_loop(act, lambda c, par: attend0(b, c, par), 2, 2)
                copy_sum(b, 0, NCH - 1, 1)
                conv1_out(b, 0)
                split_post(b, 0, NCH - 2, 0)
                conv1_out(b, 1)
                act.wait_ge(post_split, step_no(b, 0, NCH - 1) + 1)
                qk_out(b, 0)
                act.wait_ge(qk_split, b * NCH + 1)
                split_post(b, 0, NCH - 1, 1)
                act.wait_ge(post_split, step_no(b, 0, NCH) + 1)
                act.wait_ge(qk_split, b * NCH + 1)
                stage(b, 1, 0, 0)
                for c in range(2, NCH + 1):
                    if c < NCH:
                        conv1_out(b, c)
                    qk_out(b, c - 1)
                act.wait_ge(cam_step, b * 5 + 4)
                nc.scalar.activation(ex[:, :], en[:, :], ACT.Exp, bias=st[:, 2:3],
                                     accum_out=st[:, 3:4]).then_inc(cam_exp, 1)
                row(b, 1, 0, 0, 1)
                for c in range(NCH):
                    act.wait_ge(cam_ready, b * NCH + c + 1)
                    if c >= 2:
                        act.wait_ge(cam_split, b * NCH + (c - 1))
                    else:
                        act.wait_ge(qk_split, b * NCH + NCH)
                    affine(coarse[:, c % 2, :].bitcast(F32R), work[:, c % 4, :],
                           scale=col[:, MASK_HALF:MASK_HALF + 1]).then_inc(cam_coarse, 1)
                act.wait_ge(cam_split, b * NCH + NCH)
                chunk_loop(act, lambda c, par: attend1(b, c, par), 1, 1)
                copy_num(b, NCH - 1)
                chunk_loop(act, lambda c, par: conv2_out(b, c, par), 2, 0)
                features(b, NCH - 1, 1)

        @block.vector
        def _(dve):
            v = nc.vector
            dve.sem_inc(max_done, 2)
            dve.sem_inc(num_taken, 1)
            dve.sem_inc(u_ready, 1)
            dve.sem_inc(sum_taken, 2)
            dve.sem_inc(post_split, 1)
            dve.sem_inc(branch_sum, 2)
            dve.sem_inc(out_staged, 2)
            dve.wait_ge(consts_in, 16 * N_LOADS)
            n_setup = 0

            def link(ins):
                nonlocal n_setup
                n_setup += 1
                ins.then_inc(setup_dve, 1)
                dve.wait_ge(setup_dve, n_setup)

            for k, (g, bb, m, var) in enumerate(((BN1_G, BN1_B, BN1_M, BN1_V), (BN2_G, BN2_B, BN2_M, BN2_V))):
                ins = v.tensor_scalar(bn[:, k, 0:1], col[:, var:var + 1], 1e-5, None, ALU.add)
            link(ins)
            dve.wait_ge(setup_act, 2)
            for k, (g, bb, m, var) in enumerate(((BN1_G, BN1_B, BN1_M, BN1_V), (BN2_G, BN2_B, BN2_M, BN2_V))):
                q = [bn[:, k, i:i + 1] for i in range(6)]
                link(v.reciprocal(q[2], q[1]))
                link(v.tensor_tensor(q[3], q[0], q[2], ALU.mult))
                link(v.tensor_tensor(q[3], q[3], q[1], ALU.add))
                link(v.tensor_scalar(q[3], q[3], 0.5, None, ALU.mult))
                link(v.reciprocal(q[2], q[3]))
                link(v.tensor_tensor(q[4], q[2], col[:, g:g + 1], ALU.mult))
                link(v.tensor_tensor(q[3], q[4], col[:, m:m + 1], ALU.mult))
                link(v.tensor_tensor(q[5], col[:, bb:bb + 1], q[3], ALU.subtract))
            v.tensor_scalar(neg_idn[:], idn[:], -1.0, None, ALU.mult)
            v.tensor_scalar(proj_y[C:96, :], proj_y[C:96, :], col[C:96, GAMMA0:GAMMA0 + 1], None, ALU.mult)
            v.tensor_scalar(proj_p[C:P, :], proj_p[C:P, :], col[C:P, GAMMA_PA:GAMMA_PA + 1], None, ALU.mult)
            link(v.tensor_tensor(bv_g[:, 0:1], col[:, B_V:B_V + 1], col[:, GAMMA_PA:GAMMA_PA + 1], ALU.mult))
            v.tensor_tensor(bv_g[:, 1:2], bv_g[:, 0:1], col[:, MASK_HALF:MASK_HALF + 1], ALU.mult)
            v.tensor_tensor(bqk_m[:, :], col[0:C, B_QK:B_QK + 1], col[0:C, MASK_QK:MASK_QK + 1], ALU.mult)
            c1 = wtmp[:, 0:TAPS * P].rearrange("p (t m) -> p t m", t=TAPS)
            link(v.tensor_copy(w1[:, 0, :, :], c1))
            link(v.tensor_tensor(w1[:, 1, :, :], c1, w1[:, 0, :, :].bitcast(F32), ALU.subtract))
            for w, off, hi in ((w2p, TAPS * P, 0), (w2c, TAPS * (P + C), 1)):
                src = wtmp[:, off:off + TAPS * C].rearrange("p (t m) -> p t m", t=TAPS)
                a, f = w[:, :, hi * C:(hi + 1) * C], w[:, :, (1 - hi) * C:(2 - hi) * C]
                link(v.tensor_copy(a, src))
                link(v.tensor_tensor(f, src, a.bitcast(F32), ALU.subtract))
            v.memset(y_pad[:].bitcast(F32), 0.0)
            v.memset(c_pad[:].bitcast(F32), 0.0)
            v.memset(keys[:, :].bitcast(F32), 0.0)
            for t in (x_in[C:P, :], qs[:, :, :].bitcast(F32), mx_cols[:, :, :, :], wi0[C:P, :], wqk[C:P, :], qall[32:C, :],
                      proj_y[96:P, :], cam_w[0:C, :]):
                v.memset(t, 0.0)
            v.memset(ones[:, :], 1.0)
            link(v.memset(gt[:, :, 0:C2], 1.0))
            v.memset(keys[32:34, :].bitcast(F32), 1.0).then_inc(consts_ready, 1)

            def take_max(b, layer, c, par, u, bank):
                n = TILES[layer] // QT
                lt, kc = u if isinstance(u, tuple) else (u // n, u % n)
                if isinstance(u, tuple):
                    u = kc * QT + lt
                dve.wait_ge(smax_ready, tile_no(b, layer, c, u + 1))
                v.tensor_reduce(mx[:, par, lt, kc:kc + 1], ring[:, bank, :], AX.X, ALU.max).then_inc(max_done, 1)

            def finish_max(b, layer, c, par):
                n = TILES[layer] // QT
                at = step_no(b, layer, c) * 2
                dve.wait_ge(max_done, tile_no(b, layer, c + 1, 2))
                v.tensor_reduce(mx1[:, par, :], mx[:, par, :, 0:n], AX.X, ALU.max).then_inc(mx_step, 1)
                dve.wait_ge(mx_step, at + 1)
                v.tensor_copy(mx_cols[:, par, :, 0].bitcast(F32R), mx1[:, par, :]).then_inc(mx_step, 1)
                dve.wait_ge(mx_step, at + 2)
                v.tensor_tensor(mx_cols[:, par, :, 1], mx1[:, par, :], mx_cols[:, par, :, 0],
                                ALU.subtract).then_inc(mx_ready, 1)

            def take_num(b, c):
                dve.wait_ge(num_half, b * NCH + (c + 1))
                dve.wait_ge(u_ready, step_no(b, 1, c) + 1)
                v.tensor_tensor(wnum[C:P, :], acc[0:C, 0, :], half_num[:, :], ALU.add).then_inc(num_taken, 1)

            def take_sum(b, layer, c, par):
                dve.wait_ge(sum_half, step_no(b, layer, c) + 1)
                dve.wait_ge(u_ready, step_no(b, layer, c) + 1)
                v.tensor_tensor(sums[:, :], acc[0:C, par if layer == 0 else 1, :], half_sum[:, :],
                                ALU.add).then_inc(sum_taken, 1)

            def normalise(b, layer, c, stages=(0, 1, 2, 3)):
                n = (C2, C)[layer]
                lo, hi = n, 2 * n
                at = step_no(b, layer, c) * 3
                if 0 in stages:
                    dve.wait_ge(sum_taken, step_no(b, layer, c) + 1 + 2)
                    v.transpose(inv_t[0:n, :], sums[0:n, :]).then_inc(norm_step, 1)
                if 1 in stages:
                    dve.wait_ge(norm_step, at + 1)
                    v.reciprocal(inv_c[lo:hi, :], inv_t[0:n, 0:CHUNK:32]).then_inc(norm_step, 1)
                if 2 in stages:
                    dve.wait_ge(norm_step, at + 2)
                    v.transpose(inv[lo:hi, :].rearrange("p (a b) -> p a b", b=32),
                                inv_c[lo:hi, :].unsqueeze(2).to_broadcast([n, CHUNK // 32, 32])).then_inc(norm_step, 1)
                if 3 in stages and layer == 1:
                    dve.wait_ge(norm_step, at + 3)
                    dve.wait_ge(num_taken, b * NCH + (c + 1 + 1))
                    v.tensor_tensor(pc[C:P, chunk(c)], wnum[lo:hi, :], inv[lo:hi, :], ALU.mult).then_inc(u_ready, 1)

            def split_post(b, layer, c, odd):
                dve.wait_ge(post_coarse, step_no(b, layer, c) + 1)
                o = image_rows(y_pad, c)
                i, g = (a.rearrange("p (r w) -> p r w", w=W) for a in (post_out(layer, c, odd), coarse[:, 0, :]))
                if layer == 0:
                    v.tensor_tensor(o, i, g, ALU.subtract).then_inc(post_split, 1)
                else:
                    v.scalar_tensor_tensor(out=o, in0=i, scalar=bv_g[:, 0:1], in1=g, op0=ALU.add,
                                           op1=ALU.subtract).then_inc(post_split, 1)

            def attend0(b, c, par):
                nxt = not is_last(c)

                def units(*us):
                    for u in us:
                        if nxt:
                            take_max(b, 0, c + 1, 1 - par, u, u % 2)
                def before(stage):
                    if not early(c, 2):
                        normalise(b, 0, c - 2, (stage,))
                before(0)
                if not early(c, 3):
                    split_post(b, 0, c - 3, 1 - par)
                units(0)
                before(1)
                before(2)
                units(1, 2)
                if not early(c, 1):
                    take_sum(b, 0, c - 1, 1 - par)
                units(3, 4, 5, 6, 7)
                if nxt:
                    finish_max(b, 0, c + 1, 1 - par)
                else:
                    normalise(b, 0, c - 1)

            def attend1(b, c, par):
                nxt, before = not is_last(c), not early(c, 1)
                for u in range(FIRST_UNIT[GROUPS]):
                    if nxt:
                        take_max(b, 1, c + 1, 1 - par, u, (u + (u >= POST_UNIT)) % 2)
                    if before:
                        if u == 4:
                            take_num(b, c - 1)
                        if u == FIRST_UNIT[2] + 3:
                            take_sum(b, 1, c - 1, 1 - par)
                        for stage, after in enumerate((0, 1, 2, 4)):
                            if u == FIRST_UNIT[3] + after:
                                normalise(b, 1, c - 1, (stage,))
                        if u == POST_UNIT:
                            split_post(b, 1, c - 1, 1 - par)
                if nxt:
                    finish_max(b, 1, c + 1, 1 - par)

            def branch(b, c, par):
                dve.wait_ge(part_ready, b * NCH + (c + 1))
                dve.wait_ge(feat_ready, b * NCH + (c + 1))
                v.tensor_tensor(bsum[0:C, par, :], work[0:C, par, :], part[0:C, par, :], ALU.add)
                v.tensor_tensor(bsum[C:P, par, :], work[C:P, 2 + par, :], part[C:P, par, :],
                                ALU.add).then_inc(branch_sum, 1)
                if early(c, 1):
                    take_sum(b, 1, NCH - 1, 1)
                    normalise(b, 1, NCH - 1)
                else:
                    stage_out(b, c - 1, 1 - par)
                    if early(c, 2):
                        split_post(b, 1, NCH - 1, 1)
                in0(b + 1, c, par)

            def stage_out(b, c, par):
                dve.wait_ge(out_ready, b * NCH + (c + 1 + 2))
                dve.wait_ge(out_stored[par], b * (8 * NCH) + (c * 8 + (8 if par else 16)) )
                v.tensor_scalar(ostage[:, par, :], ring[0:C, par, :], col[0:C, B_OUT:B_OUT + 1], None,
                                ALU.add).then_inc(out_staged, 1)

            def in0(b, c, par):
                dve.wait_ge(in0_ready, b * NCH + (c + 1))
                v.tensor_reduce(pooled[C:P, bass.ds(c * P, P)].rearrange("p (a k) -> p a k", a=ROWS // 2),
                                acc[C:P, par, :].rearrange("p (a r k q) -> p a k r q", a=ROWS // 2, r=2, q=2),
                                AX.XY, ALU.max).then_inc(pool_done, 1)
                dve.wait_ge(theta_coarse, b * NCH + (c + 1))
                v.tensor_tensor(qall[0:32, chunk(c)].bitcast(F32R), acc[0:32, par, :], coarse[0:32, par, :],
                                ALU.subtract).then_inc(in0_used, 1)
                dve.wait_ge(phi_coarse, b * NCH + (c + 1))
                v.tensor_tensor(keys[0:32, bass.ds(c * P, P)], pooled[C:96, bass.ds(c * P, P)],
                                coarse[C:96, par, 0:P], ALU.subtract).then_inc(phi_split, 1)

            chunk_loop(dve, lambda c, par: in0(0, c, par), 2, 0)
            with dve.Fori(0, B) as b:
                for u in range(TILES[0]):
                    take_max(b, 0, 0, 0, (u % QT, u // QT), u % 2)
                finish_max(b, 0, 0, 0)
                dve.wait_ge(gt_ready, b + 1)
                v.tensor_copy(gt[:, :, C2:2 * C2], acc[:, 0, 0:TILES[0] * 32].rearrange("p (t c) -> p t c", c=32))\
                    .then_inc(gt_copied, 1)
                chunk_loop(dve, lambda c, par: attend0(b, c, par), 3, 1)
                split_post(b, 0, NCH - 3, 1)
                take_sum(b, 0, NCH - 1, 1)
                normalise(b, 0, NCH - 1)
                split_post(b, 0, NCH - 2, 0)

                def qk_out(c):
                    dve.wait_ge(qk_coarse, b * NCH + c + 1)
                    for o, r in ((qall[0:32, chunk(c)].bitcast(F32R), slice(0, 32)), (keys[0:32, chunk(c)], slice(32, C))):
                        last = v.scalar_tensor_tensor(out=o, in0=work[r, 2 + c % 2, :], scalar=col[r, B_QK:B_QK + 1],
                                                      in1=coarse[r, c % 2, :], op0=ALU.add, op1=ALU.subtract)
                    last.then_inc(qk_split, 1)

                def transposed(c):
                    dve.wait_ge(tr_ready, b * NCH + c + 1)
                    v.tensor_copy(pt_ct[:, QT * c:QT * (c + 1), :],
                                  acc[:, 1, :].rearrange("p (t c) -> p t c", t=QT)).then_inc(tr_copied, 1)

                qk_out(0)
                transposed(0)
                split_post(b, 0, NCH - 1, 1)
                for c in range(2, NCH + 1):
                    ahead = QT if c < NCH else 2
                    for lt in range(ahead):
                        take_max(b, 1, 0, 0, (lt, c - 2), lt % 2)
                    qk_out(c - 1)
                    transposed(c - 1)
                    for lt in range(ahead, QT):
                        take_max(b, 1, 0, 0, (lt, c - 2), lt % 2)
                e = acc[0:C, 0, 0:C]
                last_keys = NCH - 1
                dve.wait_ge(energy_ready, b + 1)
                v.tensor_reduce(st[:, 0:1], e, AX.X, ALU.max).then_inc(cam_step, 1)
                take_max(b, 1, 0, 0, (0, last_keys), 0)
                dve.wait_ge(cam_step, b * 5 + 1)
                v.tensor_scalar(en[:, :], e, st[:, 0:1], -1.0, ALU.subtract, ALU.mult).then_inc(cam_step, 1)
                take_max(b, 1, 0, 0, (1, last_keys), 1)
                dve.wait_ge(cam_step, b * 5 + 2)
                v.tensor_reduce(st[:, 1:2], en[:, :], AX.X, ALU.max).then_inc(cam_step, 1)
                take_max(b, 1, 0, 0, (2, last_keys), 0)
                dve.wait_ge(cam_step, b * 5 + 3)
                v.tensor_scalar(st[:, 2:3], st[:, 1:2], -1.0, None, ALU.mult).then_inc(cam_step, 1)
                take_max(b, 1, 0, 0, (3, last_keys), 1)
                finish_max(b, 1, 0, 0)
                dve.wait_ge(cam_exp, b + 1)
                v.reciprocal(st[:, 4:5], st[:, 3:4]).then_inc(cam_step, 1)
                dve.wait_ge(cam_step, b * 5 + 5)
                for k in range(2):
                    last = v.tensor_scalar(attn[:, k, :], ex[:, :], st[:, 4:5],
                                           col[0:C, GAMMA_CA:GAMMA_CA + 1], ALU.mult, ALU.mult)
                last.then_inc(attn_ready, 1)
                dve.wait_ge(attn_t_ready, b + 1)
                v.tensor_tensor(cam_w[C:P, :], acc[C:P, 1, 0:P], two_idn[C:P, :], ALU.add).then_inc(cam_w_ready, 1)
                for c in range(NCH):
                    dve.wait_ge(cam_coarse, b * NCH + c + 1)
                    v.tensor_tensor(image_rows(c_pad, c), work[:, c % 4, :].rearrange("p (r w) -> p r w", w=W),
                                    coarse[:, c % 2, :].rearrange("p (r w) -> p r w", w=W),
                                    ALU.subtract).then_inc(cam_split, 1)
                chunk_loop(dve, lambda c, par: attend1(b, c, par), 1, 1)
                take_num(b, NCH - 1)
                chunk_loop(dve, lambda c, par: branch(b, c, par), 2, 0)
                stage_out(b, NCH - 1, 1)


N_LOADS = 18


def kernel(**inputs):
    import numpy as np
    import concourse.bacc as bacc
    from concourse.bass_utils import run_bass_kernel_spmd

    g = {k: np.ascontiguousarray(v) for k, v in inputs.items()}
    f = np.float32

    def l1(name):
        return g["L1_conv_" + name]

    zero = np.zeros((C, 32), f)
    w_in0 = np.concatenate([np.tile(g["L0_conv_w_theta"].T, (1, 4)), zero, np.tile(g["L0_conv_w_phi"].T, (1, 4)),
                            g["L0_conv_w_g"].T], axis=1)
    w_o0 = np.tile(g["L0_conv_w_o"].T, (1, 2))
    w_qk = np.concatenate([np.tile(l1("wq").T, (1, 4)), np.tile(l1("wk").T, (1, 4))], axis=1)
    w_v = np.tile(l1("wv").T, (1, 2))

    def taps(w):
        return w.transpose(1, 2, 3, 0).reshape(C, TAPS, C)

    w_c1 = np.tile(np.concatenate([taps(l1("w_pam1")), taps(l1("w_cam1"))], axis=2), (2, 1, 1)).reshape(P, TAPS * P)
    w_c2p = np.tile(taps(l1("w_pam2")), (2, 1, 1)).reshape(P, TAPS * C)
    w_c2c = np.tile(taps(l1("w_cam2")), (2, 1, 1)).reshape(P, TAPS * C)
    w_out = np.tile(l1("w_out").T, (2, 1))
    cols = np.zeros((P, NCOL), f)
    for k, n in ((0, "1"), (4, "2")):
        for i, s in enumerate("gbmv"):
            cols[:, k + i] = np.concatenate([l1(f"bn_pam{n}_{s}"), l1(f"bn_cam{n}_{s}")])
    cols[:C, B_QK] = np.concatenate([np.tile(l1("bq"), 4), np.tile(l1("bk"), 4)])
    cols[:, B_V] = np.tile(l1("bv"), 2)
    cols[:C, B_OUT] = l1("b_out")
    cols[:, GAMMA0] = g["L0_conv_gamma"]
    cols[:, GAMMA_PA] = l1("gamma_pa")
    cols[:, GAMMA_CA] = l1("gamma_ca")
    cols[C:, MASK_HALF] = 1
    group = np.arange(32) // C8
    cols[:32, MASK_QK] = group // 2
    cols[32:64, MASK_QK] = group % 2
    cols[64:96, MASK_QK] = group % 2
    arrays = {"x": g["x"].reshape(B, C, L), "cols": cols, "ident": np.eye(P, dtype=f), "w_in0": w_in0, "w_o0": w_o0,
              "w_qk": w_qk, "w_v": w_v, "w_c1": w_c1, "w_c2p": w_c2p, "w_c2c": w_c2c, "w_out": w_out}
    arrays = {f"in_{k}": np.ascontiguousarray(a) for k, a in arrays.items()}
    nc = bacc.Bacc("TRN2", target_bir_lowering=False, num_devices=1)
    args = [nc.dram_tensor(k, a.shape, mybir.dt.from_np(a.dtype), kind="ExternalInput").ap() for k, a in arrays.items()]
    args.append(nc.dram_tensor("out_0", (B, C, L), F32, kind="ExternalOutput").ap())
    build(nc, *args)
    r = run_bass_kernel_spmd(nc, [arrays], core_ids=[0])
    return r.results[0]["out_0"].reshape(B, C, H, W)
```

```python
from contextlib import ExitStack

import concourse.bass as bass
from concourse import mybir

ALU = mybir.AluOpType
ACT = mybir.ActivationFunctionType
AX = mybir.AxisListType
F32 = mybir.dt.float32
F32R = mybir.dt.float32r

B, C, H, W = 16, 64, 64, 64
L = H * W
P = 128
CHUNK = 512
NCH = L // CHUNK
ROWS = CHUNK // W
QT = CHUNK // P
HP, WP = H + 2, W + 2
TAPS = 9
C8, C2 = C // 8, C // 2
KEYS = (L // 4, L)
TILES = (KEYS[0] // P, KEYS[1] // P)
TILE_OFF = (0, TILES[0] * NCH)
GROUP = 4
GROUPS = TILES[1] // GROUP
PAIRS = (TILES[0] // 2, TILES[1] // 2)
PAIRS_ALL = (PAIRS[0] + PAIRS[1]) * NCH
TILES_ALL = (TILES[0] + TILES[1]) * NCH
STEPS = 2 * NCH
RING0 = ((0, None), (1, None), (0, 0), (1, 1), (0, 2), (2, None), (1, 3), (0, 4))
UNITS = (4, 5, 4, 5, 5, 4, 4, 1)
FIRST_UNIT = tuple(sum(UNITS[:g]) for g in range(GROUPS + 1))
POST_GROUP = 5
POST_UNIT = FIRST_UNIT[POST_GROUP] + 1
CAM_GROUP = 6
CAM_UNIT = FIRST_UNIT[CAM_GROUP] + 1
NUM_UNIT, LAST_OCT_UNIT, SUM_UNIT, NORM_UNITS, OCT_UNITS = 3, 5, 11, (12, 13, 15, 17), (23, 27)


def plan_ring():
    order, had, plan = [0, 1], {0: None, 1: None, 2: None}, {}
    for u in range(sum(UNITS)):
        if u == FIRST_UNIT[3]:
            order.insert(0, 2)
        for user in ["post"] * (u == POST_UNIT) + ["cam"] * (u == CAM_UNIT) + [u]:
            bank = order.pop(0)
            order.append(bank)
            plan[user] = (bank, had[bank])
            had[bank] = user
    return plan


RING = plan_ring()
(BN1_G, BN1_B, BN1_M, BN1_V, BN2_G, BN2_B, BN2_M, BN2_V, B_QK, B_V, B_OUT, GAMMA0, GAMMA_PA, GAMMA_CA,
 MASK_HALF, MASK_QK) = range(16)
NCOL = 16


def build(nc, x, cols, ident, w_in0, w_o0, w_qk, w_v, w_c1, w_c2p, w_c2c, w_out, out):
    ctx = ExitStack()
    with ctx:
        def sb(name, shape, dt=F32):
            return ctx.enter_context(nc.sbuf_tensor(name, shape, dt))

        def sem(name):
            return ctx.enter_context(nc.semaphore(name))

        work = ctx.enter_context(nc.psum_tensor("work", [P, 4, CHUNK], F32))
        ring = ctx.enter_context(nc.psum_tensor("ring", [P, 2, CHUNK], F32))
        acc = ctx.enter_context(nc.psum_tensor("acc", [P, 2, CHUNK], F32))

        col = sb("col", [P, NCOL])
        idn = sb("idn", [P, P])
        neg_idn = sb("neg_idn", [P, P])
        two_idn = sb("two_idn", [P, P])
        wi0 = sb("wi0", [P, P])
        proj_y = sb("proj_y", [P, P])
        proj_p = sb("proj_p", [P, P])
        wqk = sb("wqk", [P, C])
        w1 = sb("w1", [P, 2, TAPS, P], F32R)
        w2p = sb("w2p", [P, TAPS, P], F32R)
        w2c = sb("w2c", [P, TAPS, P], F32R)
        wout = sb("wout", [P, C])
        bn = sb("bn", [P, 2, 6])
        bqk_m = sb("bqk_m", [C, 1])
        bv_g = sb("bv_g", [P, 2])

        x_in = sb("x_in", [P, L])
        y_pad = sb("y_pad", [P, HP, WP], F32R)
        c_pad = sb("c_pad", [P, HP, WP], F32R)
        pc = sb("pc", [P, L])
        pt_ct = sb("pt_ct", [P, TILES[1], 2 * C])
        gt = sb("gt", [P, TILES[0], 2 * C2])
        ones = sb("ones", [P, C])
        keys = sb("keys", [P, L], F32R)
        qall = sb("qall", [C, L])
        qs = sb("qs", [P, 2, CHUNK], F32R)
        pooled = sb("pooled", [P, KEYS[0]])
        probs = sb("probs", [P, 2 * GROUP, CHUNK])
        duos = sb("duos", [P, 2, CHUNK])
        quads = sb("quads", [P, 4, CHUNK])
        octs = sb("octs", [P, 4, CHUNK])
        upper_lower = sb("upper_lower", [P, 2, CHUNK])
        half_num = upper_lower[0:C, 0, :]
        inv_t = upper_lower[0:C, 1, :]
        ostage = upper_lower[C:P, :, :]
        half_sum = sb("half_sum", [C, CHUNK])
        sums = sb("sums", [C, CHUNK])
        wnum = sb("wnum", [P, CHUNK])
        inv_c = sb("inv_c", [P, CHUNK // 32])
        inv = sb("inv", [P, CHUNK])
        mx = sb("mx", [P, 2, QT, 8])
        mx1 = sb("mx1", [P, 2, QT])
        mx_cols = sb("mx_cols", [P, 2, QT, 32])
        coarse = sb("coarse", [P, 2, CHUNK])
        part = sb("part", [P, 2, CHUNK])
        bsum = probs[:, 0:2, :]
        feat = probs[:, 2:4, :]
        en = sb("en", [C, C])
        ex = sb("ex", [C, C])
        attn = sb("attn", [C, 2, C])
        cam_w = sb("cam_w", [P, P])
        st = sb("st", [C, 6])
        wtmp = pc

        consts_in = sem("consts_in")
        consts_ready = sem("consts_ready")
        keys_zero = sem("keys_zero")
        y_zero = sem("y_zero")
        setup_act = sem("setup_act")
        setup_dve = sem("setup_dve")
        x_loaded = sem("x_loaded")
        in0_ready = sem("in0_ready")
        theta_coarse = sem("theta_coarse")
        in0_used = sem("in0_used")
        phi_coarse = sem("phi_coarse")
        pool_done = sem("pool_done")
        phi_split = sem("phi_split")
        gt_ready = sem("gt_ready")
        gt_copied = sem("gt_copied")
        staged = sem("staged")
        smax_ready = sem("smax_ready")
        max_done = sem("max_done")
        mx_step = sem("mx_step")
        mx_ready = sem("mx_ready")
        row_ready = sem("row_ready")
        row_in = sem("row_in")
        scores_ready = sem("scores_ready")
        exp_done = sem("exp_done")
        probs_used = sem("probs_used")
        duo_ready = sem("duo_ready")
        quad_ready = sem("quad_ready")
        oct_ready = sem("oct_ready")
        ones_done = sem("ones_done")
        num_half = sem("num_half")
        sum_half = sem("sum_half")
        num_taken = sem("num_taken")
        sum_taken = sem("sum_taken")
        norm_step = sem("norm_step")
        u_ready = sem("u_ready")
        post_ready = sem("post_ready")
        post_coarse = sem("post_coarse")
        post_split = sem("post_split")
        conv1_ready = sem("conv1_ready")
        pc_ready = sem("pc_ready")
        tr_ready = sem("tr_ready")
        tr_copied = sem("tr_copied")
        energy_ready = sem("energy_ready")
        cam_step = sem("cam_step")
        cam_exp = sem("cam_exp")
        attn_ready = sem("attn_ready")
        attn_t_ready = sem("attn_t_ready")
        cam_w_ready = sem("cam_w_ready")
        qk_ready = sem("qk_ready")
        qk_coarse = sem("qk_coarse")
        qk_split = sem("qk_split")
        cam_ready = sem("cam_ready")
        cam_coarse = sem("cam_coarse")
        cam_split = sem("cam_split")
        conv2_ready = sem("conv2_ready")
        part_ready = sem("part_ready")
        branch_sum = sem("branch_sum")
        feat_ready = sem("feat_ready")
        out_ready = sem("out_ready")
        out_staged = sem("out_staged")
        out_stored = [sem(f"out_stored{i}") for i in range(2)]

        def tile_no(b, layer, c, u):
            return b * TILES_ALL + c * TILES[layer] + (layer * NCH * TILES[0] + u)

        def pair_no(b, layer, c, q):
            return b * PAIRS_ALL + c * PAIRS[layer] + (layer * NCH * PAIRS[0] + q)

        def step_no(b, layer, c):
            return b * STEPS + (c + NCH * layer)

        def chunk(c):
            return bass.ds(c * CHUNK, CHUNK)

        def image_rows(tile, c):
            return tile[:, bass.ds(c * ROWS + 1, ROWS), 1:1 + W]

        def chunk_loop(eng, step, before, after):
            for c in range(before):
                step(c, c % 2)
            with eng.Fori(0, (NCH - before - after) // 2) as turn:
                for k in range(2):
                    step(turn * 2 + (before + k), (before + k) % 2)
            for c in range(NCH - after, NCH):
                step(c, c % 2)

        def post_out(layer, c, odd):
            if layer == 0:
                return acc[:, 1 - odd, :]
            return ring[:, 1, :] if is_last(c) else ring_bank("post")

        def ring_bank(user):
            bank = RING[user][0]
            return ring[:, bank, :] if bank < 2 else acc[:, 1, :]

        def ring_bank0(u, par):
            bank = RING0[u][0]
            return ring[:, bank, :] if bank < 2 else acc[:, 1 - par, :]

        def early(c, n):
            return isinstance(c, int) and c < n

        def is_last(c):
            return isinstance(c, int) and c == NCH - 1

        def settle(eng):
            eng.wait_ge(consts_ready, 2)

        block = ctx.enter_context(nc.Block())

        @block.sync
        def _(sp):
            loads = [(col[:], cols), (idn[:], ident), (two_idn[0:C, 0:C], ident[0:C, 0:C]),
                     (two_idn[0:C, C:P], ident[0:C, 0:C]), (two_idn[C:P, 0:C], ident[0:C, 0:C]),
                     (two_idn[C:P, C:P], ident[0:C, 0:C]), (wi0[0:C, :], w_in0), (proj_y[C:96, :], w_o0),
                     (proj_p[C:P, :], w_v), (wqk[0:C, :], w_qk), (wtmp[:, 0:TAPS * P], w_c1),
                     (wtmp[:, TAPS * P:TAPS * (P + C)], w_c2p), (wtmp[:, TAPS * (P + C):TAPS * 2 * P], w_c2c),
                     (wout[:], w_out), (proj_y[0:C, 0:C], ident[0:C, 0:C]), (proj_y[0:C, C:P], ident[0:C, 0:C]),
                     (proj_p[0:C, 0:C], ident[0:C, 0:C]), (proj_p[0:C, C:P], ident[0:C, 0:C])]
            assert len(loads) == N_LOADS
            for dst, src in loads:
                sp.dma_start(dst, src).then_inc(consts_in, 16)
            for s in out_stored:
                sp.sem_inc(s, 16)
            sp.dma_start(x_in[0:C, :], x[0]).then_inc(x_loaded, 16)

            def store(b, c, par):
                sp.wait_ge(out_staged, b * NCH + (c + 1 + 2))
                sp.dma_start(out_view(b, c), ostage[:, par, :]).then_inc(out_stored[par], 16)

            def out_view(b, c):
                return out[bass.ds(b, 1), :, chunk(c)].rearrange("o c l -> (o c) l")

            def stores(b):
                chunk_loop(sp, lambda c, par: store(b, c, par), 0, 0)

            with sp.Fori(0, B - 1) as b:
                sp.wait_ge(post_ready, b * STEPS + NCH)
                sp.dma_start(x_in[0:C, :], x[bass.ds(b + 1, 1)].rearrange("o c l -> (o c) l")).then_inc(x_loaded, 16)
                stores(b)
            sp.wait_ge(post_ready, (B - 1) * STEPS + NCH)
            sp.dma_start(x_in[0:C, :], x[B - 1]).then_inc(x_loaded, 16)
            stores(B - 1)
            for s in out_stored:
                sp.wait_ge(s, 16 + B * NCH // 2 * 16)

        @block.gpsimd
        def _(pool):
            pool.sem_inc(quad_ready, 2)
            nc.gpsimd.memset(y_pad[:].bitcast(F32), 0.0).then_inc(y_zero, 1)
            pool.wait_ge(y_zero, 1)
            nc.gpsimd.memset(c_pad[:].bitcast(F32), 0.0).then_inc(consts_ready, 1)

            def quad(b, c, g):
                at = b * (NCH * GROUPS) + (c * GROUPS + g)
                slot = GROUP * (g % 2)
                pool.wait_ge(exp_done, pair_no(b, 1, c, 2 * g + 2 + 2))
                pool.wait_ge(quad_ready, at + 2)
                nc.gpsimd.tensor_tensor(duos[:, :, :], probs[:, slot:slot + 2, :], probs[:, slot + 2:slot + 4, :],
                                        ALU.add).then_inc(duo_ready, 1)
                if g % 2 == 0:
                    pool.wait_ge(oct_ready, b * (NCH * GROUPS // 2) + (c * (GROUPS // 2) + g // 2 + 1))
                pool.wait_ge(duo_ready, at + 1)
                nc.gpsimd.tensor_tensor(quads[:, g % 4, :], duos[:, 0, :], duos[:, 1, :],
                                        ALU.add).then_inc(quad_ready, 1)

            def divide(b, c):
                pool.wait_ge(norm_step, step_no(b, 0, c) * 3 + 3)
                nc.gpsimd.tensor_tensor(x_in[C:96, chunk(c)], sums[C2:C, :], inv[C2:C, :], ALU.mult)\
                    .then_inc(u_ready, 1)

            with pool.Fori(0, B) as b:
                with pool.Fori(0, NCH) as c:
                    divide(b, c)
                with pool.Fori(0, NCH) as c:
                    for g in range(GROUPS):
                        quad(b, c, g)

        @block.tensor
        def _(pe):
            def mm(o, a, r, start=True, stop=True):
                return nc.tensor.matmul(o, a, r, start=start, stop=stop)

            pe.sem_inc(probs_used, 4)
            pe.sem_inc(ones_done, 2)
            pe.sem_inc(out_ready, 2)
            pe.wait_ge(consts_ready, 2)

            def max_unit(b, layer, c, par, u, bank, before=None):
                n = TILES[layer] // QT
                lt, kc = u if isinstance(u, tuple) else (u // n, u % n)
                if before is not None:
                    pe.wait_ge(max_done, tile_no(b, layer, c, before + 1 + 2))
                mm(ring[:, bank, :] if isinstance(bank, int) else bank, qs[:, par, lt * P:(lt + 1) * P],
                   keys[:, kc * CHUNK:(kc + 1) * CHUNK]).then_inc(smax_ready, 1)

            def max_row(b, layer, c, par, bank):
                pe.wait_ge(mx_ready, step_no(b, layer, c) + 1)
                for lt in range(QT):
                    last = mm(ring[0:32, bank, lt * P:(lt + 1) * P], mx_cols[:, par, lt, :], neg_idn[:, :])
                last.then_inc(row_ready, 1)

            def project(b, layer, c, odd):
                pe.wait_ge(u_ready, step_no(b, layer, c) + 1 + 1)
                w, r = (proj_y, x_in) if layer == 0 else (proj_p, pc)
                mm(post_out(layer, c, odd), w[:, :], r[:, chunk(c)]).then_inc(post_ready, 1)

            def score_pair(b, layer, c, par, q):
                pe.wait_ge(exp_done, pair_no(b, layer, c, q + 1))
                for t in (2 * q, 2 * q + 1):
                    last = mm(work[:, t % 4, :], keys[:, t * P:(t + 1) * P], qs[:, par, :])
                last.then_inc(scores_ready, 1)

            def weigh_pair(b, layer, c, par, q):
                pe.wait_ge(exp_done, pair_no(b, layer, c, q + 1 + 2))
                if q == 0 and layer == 0:
                    pe.wait_ge(sum_taken, step_no(b, 0, c) + 1)
                    if not early(c, 2):
                        pe.wait_ge(post_split, step_no(b, 0, c) - 2 + 1)
                if q == 0 and layer == 1:
                    pe.wait_ge(num_taken, b * NCH + (c + 1))
                for t in (2 * q, 2 * q + 1):
                    h = C * (t % 2)
                    w, bank = (gt[:, t, :], par) if layer == 0 else (pt_ct[:, t, 0:C], 0)
                    last = mm(acc[h:h + C, bank, :], w, probs[:, t % 8, :], start=(q == 0),
                              stop=(q == PAIRS[layer] - 1))
                last.then_inc(probs_used, 1)

            def sum_pair(b, c, k):
                pe.wait_ge(oct_ready, b * (NCH * GROUPS // 2) + (c * (GROUPS // 2) + 2 * k + 2 + 2))
                if k == 0:
                    pe.wait_ge(sum_taken, step_no(b, 1, c) + 2)
                for h in range(2):
                    last = mm(acc[C * h:C * h + C, 1, :], ones[:, :], octs[:, 2 * k + h, :], start=(k == 0),
                              stop=(k == 1))
                last.then_inc(ones_done, 1)

            def attend0(b, c, par):
                nxt = not is_last(c)

                def unit(u):
                    if nxt:
                        if u == 5 and not early(c, 1):
                            pe.wait_ge(sum_taken, step_no(b, 0, c) + 2)
                        max_unit(b, 0, c + 1, 1 - par, u, ring_bank0(u, par), RING0[u][1])
                if nxt:
                    pe.wait_ge(staged, step_no(b, 0, c) + 2)
                unit(0)
                pe.wait_ge(row_in, step_no(b, 0, c) + 1)
                score_pair(b, 0, c, par, 0)
                unit(1)
                score_pair(b, 0, c, par, 1)
                unit(2)
                weigh_pair(b, 0, c, par, 0)
                unit(3)
                score_pair(b, 0, c, par, 2)
                unit(4)
                weigh_pair(b, 0, c, par, 1)
                unit(5)
                score_pair(b, 0, c, par, 3)
                unit(6)
                unit(7)
                weigh_pair(b, 0, c, par, 2)
                if not early(c, 2):
                    if nxt:
                        pe.wait_ge(max_done, tile_no(b, 0, c + 1, 5 + 1 + 2))
                    else:
                        pe.wait_ge(sum_taken, step_no(b, 0, c) + 2)
                    project(b, 0, c - 2, par)
                if nxt:
                    max_row(b, 0, c + 1, 1 - par, 1)
                weigh_pair(b, 0, c, par, 3)

            def attend1(b, c, par):
                nxt, before = not is_last(c), not early(c, 1)
                if nxt:
                    pe.wait_ge(staged, step_no(b, 1, c) + 2)

                def ring_free(user):
                    bank, had = RING[user]
                    if bank == 2 and had is None and before:
                        pe.wait_ge(sum_taken, step_no(b, 1, c) + 2)
                    elif bank == 2 and had is None:
                        pe.wait_ge(cam_w_ready, b + 1)
                    if had == "post" and not before:
                        had = RING["post"][1]
                    if had == "post":
                        pe.wait_ge(post_split, step_no(b, 1, c) + 1)
                    elif had == "cam":
                        pe.wait_ge(cam_split, b * NCH + (c + 1))
                    elif had is not None and nxt:
                        pe.wait_ge(max_done, tile_no(b, 1, c + 1, had + 1 + 2))

                for g in range(GROUPS):
                    units = list(range(FIRST_UNIT[g], FIRST_UNIT[g + 1])) if nxt else []

                    def unit():
                        if units:
                            u = units.pop(0)
                            ring_free(u)
                            max_unit(b, 1, c + 1, 1 - par, u, ring_bank(u))
                    post, cam = g == POST_GROUP and before, g == CAM_GROUP
                    if g == 0:
                        unit()
                        pe.wait_ge(row_in, step_no(b, 1, c) + 1)
                    score_pair(b, 1, c, par, 2 * g)
                    unit()
                    if post:
                        ring_free("post")
                        project(b, 1, c - 1, 1 - par)
                    if cam:
                        ring_free("cam")
                        mm(ring_bank("cam"), cam_w[:, :], pc[:, chunk(c)]).then_inc(cam_ready, 1)
                    if post or cam:
                        unit()
                    if g == 0 and before:
                        weigh_pair(b, 1, c - 1, 1 - par, 2 * GROUPS - 1)
                        unit()
                    score_pair(b, 1, c, par, 2 * g + 1)
                    if g == 0 and not before:
                        pe.wait_ge(attn_ready, b + 1)
                        mm(acc[:, 1, 0:P], attn[:, :, :].rearrange("c a d -> c (a d)"), two_idn[0:C, :])\
                            .then_inc(attn_t_ready, 1)
                    if not (post or cam):
                        unit()
                    if g >= 1:
                        weigh_pair(b, 1, c, par, 2 * g - 2)
                    while len(units) > 1 and not (post or cam):
                        unit()
                    if g >= 1:
                        weigh_pair(b, 1, c, par, 2 * g - 1)
                    while units:
                        unit()
                    if g == GROUPS - 1 and nxt:
                        max_row(b, 1, c + 1, 1 - par, 1)
                    if g < 2 and before:
                        sum_pair(b, c - 1, g)
                weigh_pair(b, 1, c, par, 2 * GROUPS - 2)

            def proj0(b, c, par):
                if early(c, 1):
                    pe.wait_ge(x_loaded, b * 16 + 16)
                    pe.wait_ge(num_taken, b * NCH + 1)
                elif early(c, 2):
                    pe.wait_ge(sum_taken, step_no(b, 0, 0) + 2)
                else:
                    pe.wait_ge(in0_used, b * NCH + (c - 1))
                mm(acc[:, par, :], wi0[:, :], x_in[:, chunk(c)]).then_inc(in0_ready, 1)

            def conv1(b, c, between=()):
                if c == 0:
                    pe.wait_ge(post_split, step_no(b, 0, NCH - 2) + 1)
                if c == 5:
                    pe.wait_ge(post_split, step_no(b, 0, NCH) + 1)
                if c >= 2:
                    pe.wait_ge(pc_ready, b * NCH + (c - 1))
                between = list(between)
                for i in range(2 * TAPS):
                    half, tap = divmod(i, TAPS)
                    dy, dx = divmod(tap, 3)
                    last = mm(work[:, c % 2, :], w1[:, half, tap, :],
                              y_pad[:, ROWS * c + dy:ROWS * c + dy + ROWS, dx:dx + W],
                              start=(i == 0), stop=(i == 2 * TAPS - 1))
                    if i == 2 * TAPS - 1:
                        last.then_inc(conv1_ready, 1)
                    if i % 3 == 0 and i >= TAPS and between:
                        between.pop(0)()

            def transposes(b, c):
                if c == 0:
                    pe.wait_ge(post_split, step_no(b, 0, NCH - 1) + 1)
                if c >= 1:
                    pe.wait_ge(tr_copied, b * NCH + c)
                for i in range(QT):
                    t = QT * c + i
                    last = nc.tensor.transpose(acc[:, 1, i * P:(i + 1) * P], pc[:, t * P:(t + 1) * P], idn[:, :])
                last.then_inc(tr_ready, 1)

            def energy(b, c):
                if c == 0:
                    pe.wait_ge(post_split, step_no(b, 0, NCH) + 1)
                pe.wait_ge(tr_copied, b * NCH + c + 1)
                for i in range(QT):
                    t = QT * c + i
                    ct = pt_ct[:, t, C:2 * C]
                    last = mm(acc[0:C, 0, 0:C], ct, ct, start=(t == 0), stop=(t == TILES[1] - 1))
                if c == NCH - 1:
                    last.then_inc(energy_ready, 1)

            def query_key(b, c):
                pe.wait_ge(pc_ready, b * NCH + c + 1)
                if c >= 2:
                    pe.wait_ge(qk_split, b * NCH + (c - 1))
                mm(work[0:C, 2 + c % 2, :], wqk[:, :], pc[:, chunk(c)]).then_inc(qk_ready, 1)

            def conv2(b, c, par):
                if early(c, 1):
                    pe.wait_ge(cam_split, b * NCH + NCH)
                    pe.wait_ge(post_split, step_no(b, 1, NCH - 1) + 1)
                if not early(c, 2):
                    proj0(b + 1, c, par)
                pe.wait_ge(branch_sum, b * NCH + (c + 1))

                def taps(k, pad, w):
                    for tap in range(TAPS):
                        dy, dx = divmod(tap, 3)
                        last = mm(work[:, 2 * k + par, :], w[:, tap, :],
                                  pad[:, bass.ds(c * ROWS + dy, ROWS), dx:dx + W],
                                  start=(tap == 0), stop=(tap == TAPS - 1))
                    return last
                taps(0, y_pad, w2p)
                if early(c, 2):
                    proj0(b + 1, c, par)
                if early(c, 1):
                    sum_pair(b, NCH - 1, 0)
                taps(1, c_pad, w2c).then_inc(conv2_ready, 1)
                if early(c, 1):
                    sum_pair(b, NCH - 1, 1)
                elif early(c, 2):
                    out_project(b, c - 1, 1 - par)
                    project(b, 1, NCH - 1, 1)
                else:
                    settle(pe)
                    pe.wait_ge(post_split, step_no(b, 1, NCH) + 1)
                    out_project(b, c - 1, 1 - par)

            def out_project(b, c, par):
                pe.wait_ge(feat_ready, b * NCH + (c + 1 + 2))
                pe.wait_ge(out_staged, b * NCH + (c + 1))
                mm(ring[0:C, par, :], wout[:, :], feat[:, par, :]).then_inc(out_ready, 1)

            def start0(b, output=None):
                pe.wait_ge(staged, step_no(b, 0, 0) + 1)
                pe.wait_ge(phi_split, b * NCH + NCH)
                pe.wait_ge(out_staged, b * NCH + 1)

                def unit(u):
                    max_unit(b, 0, 0, 0, (u % QT, u // QT), u % 2, u - 2 if u >= 2 else None)
                unit(0)
                unit(1)
                if output:
                    pe.wait_ge(max_done, tile_no(b, 0, 0, 2 + 2))
                    output()
                for t in range(TILES[0]):
                    last = nc.tensor.transpose(acc[:, 0, t * 32:(t + 1) * 32], pooled[96:P, t * P:(t + 1) * P],
                                               idn[96:P, 96:P])
                last.then_inc(gt_ready, 1)
                unit(2)
                if output:
                    pe.wait_ge(out_staged, b * NCH + 2)
                for u in range(3, TILES[0]):
                    unit(u)
                max_row(b, 0, 0, 0, 1)
                pe.wait_ge(gt_copied, b + 1)

            chunk_loop(pe, lambda c, par: proj0(0, c, par), 2, 0)
            start0(0)
            with pe.Fori(0, B) as b:
                chunk_loop(pe, lambda c, par: attend0(b, c, par), 2, 2)

                conv1(b, 0)
                pe.wait_ge(sum_taken, step_no(b, 0, NCH) + 2)
                project(b, 0, NCH - 2, 0)

                def first_unit(kc, lt):
                    u = kc * QT + lt
                    if u == 0:
                        pe.wait_ge(staged, step_no(b, 1, 0) + 1)
                    if lt == 0:
                        pe.wait_ge(qk_split, b * NCH + (kc + 1))
                    max_unit(b, 1, 0, 0, (lt, kc), u % 2, u - 2 if u >= 2 else None)
                for c in range(1, NCH + 2):
                    units = [lambda kc=c - 2, lt=lt: first_unit(kc, lt) for lt in range(QT)] if c >= 2 else []
                    if c < NCH:
                        conv1(b, c, units[:3])
                        for unit in units[3:]:
                            unit()
                        units = []
                    if c == NCH:
                        query_key(b, c - 1)
                        units.pop(0)()
                        units.pop(0)()
                    if c >= 2:
                        energy(b, c - 2)
                    if c < NCH:
                        query_key(b, c - 1)
                    if c <= NCH:
                        transposes(b, c - 1)
                    for unit in units:
                        unit()
                    if c == 1:
                        project(b, 0, NCH - 1, 1)
                max_row(b, 1, 0, 0, 1)
                chunk_loop(pe, lambda c, par: attend1(b, c, par), 1, 1)
                weigh_pair(b, 1, NCH - 1, 1, 2 * GROUPS - 1)
                chunk_loop(pe, lambda c, par: conv2(b, c, par), 2, 0)
                start0(b + 1, lambda: out_project(b, NCH - 1, 1))

        @block.scalar
        def _(act):
            def affine(o, i, scale=1.0, bias=0.0):
                return nc.scalar.activation(o, i, ACT.Identity, bias=bias, scale=scale)

            act.sem_inc(exp_done, 2)
            act.sem_inc(feat_ready, 2)
            act.wait_ge(setup_dve, 1)
            for k in range(2):
                nc.scalar.activation(bn[:, k, 1:2], bn[:, k, 0:1], ACT.Sqrt).then_inc(setup_act, 1)
            act.wait_ge(consts_ready, 2)

            def stage(b, layer, c, par):
                nc.scalar.copy(qs[0:C, par, :], qall[:, chunk(c)]).then_inc(staged, 1)

            def copy_num(b, c):
                act.wait_ge(probs_used, pair_no(b, 1, c + 1, 4))
                act.wait_ge(num_taken, b * NCH + (c + 1))
                nc.scalar.copy(half_num[:, :], acc[C:P, 0, :]).then_inc(num_half, 1)

            def copy_sum(b, layer, c, par):
                if layer == 0:
                    act.wait_ge(probs_used, pair_no(b, 0, c + 1, 4))
                else:
                    act.wait_ge(ones_done, b * (NCH * 2) + (c * 2 + 2 + 2))
                act.wait_ge(sum_taken, step_no(b, layer, c) + 2)
                nc.scalar.copy(half_sum[:, :], acc[C:P, par if layer == 0 else 1, :]).then_inc(sum_half, 1)

            def split_post(b, layer, c, odd):
                act.wait_ge(post_ready, step_no(b, layer, c) + 1)
                act.wait_ge(post_split, step_no(b, layer, c) + 1)
                affine(coarse[:, 0, :].bitcast(F32R), post_out(layer, c, odd), scale=col[:, MASK_HALF:MASK_HALF + 1],
                       bias=bv_g[:, 1:2] if layer else 0.0).then_inc(post_coarse, 1)

            def row(b, layer, c, par, bank):
                act.wait_ge(row_ready, step_no(b, layer, c) + 1)
                nc.scalar.copy(qs[32:C, par, :], ring[0:32, bank, :]).then_inc(row_in, 1)

            def exponentials(b, layer, c, q):
                act.wait_ge(scores_ready, pair_no(b, layer, c, q + 1))
                act.wait_ge(probs_used, pair_no(b, layer, c, q + 1))
                if layer == 1 and q % 2 == 0:
                    act.wait_ge(quad_ready, b * (NCH * GROUPS) + (c * GROUPS + q // 2 + 1))
                s = 2 * q
                nc.scalar.activation(probs[:, s % 8:s % 8 + 2, :], work[:, s % 4:s % 4 + 2, :],
                                     ACT.Exp).then_inc(exp_done, 1)

            def attend0(b, c, par):
                if not is_last(c):
                    stage(b, 0, c + 1, 1 - par)
                row(b, 0, c, par, 1)
                exponentials(b, 0, c, 0)
                if not early(c, 1):
                    copy_sum(b, 0, c - 1, 1 - par)
                exponentials(b, 0, c, 1)
                exponentials(b, 0, c, 2)
                exponentials(b, 0, c, 3)
                if not early(c, 2):
                    split_post(b, 0, c - 2, par)

            def attend1(b, c, par):
                before = not early(c, 1)
                if before:
                    if not is_last(c):
                        stage(b, 1, c + 1, 1 - par)
                    row(b, 1, c, par, 1)
                for g in range(GROUPS):
                    exponentials(b, 1, c, 2 * g)
                    if before:
                        if g == 0:
                            copy_num(b, c - 1)
                        if g == 2:
                            copy_sum(b, 1, c - 1, 1 - par)
                        if g == POST_GROUP:
                            split_post(b, 1, c - 1, 1 - par)
                    if g == CAM_GROUP:
                        act.wait_ge(cam_ready, b * NCH + (c + 1))
                        if before:
                            act.wait_ge(cam_split, b * NCH + c)
                        else:
                            act.wait_ge(qk_split, b * NCH + NCH)
                        affine(coarse[:, 1, :].bitcast(F32R), ring_bank("cam"),
                               scale=col[:, MASK_HALF:MASK_HALF + 1]).then_inc(cam_coarse, 1)
                    exponentials(b, 1, c, 2 * g + 1)

            def in0(b, c, par):
                act.wait_ge(in0_ready, b * NCH + (c + 1))
                if not early(c, 2):
                    act.wait_ge(in0_used, b * NCH + (c - 1))
                    act.wait_ge(phi_split, b * NCH + (c - 1))
                    act.wait_ge(post_split, step_no(b, 0, 0) + 1)
                elif early(c, 1) and not isinstance(b, int):
                    act.wait_ge(post_split, step_no(b, 0, 0))
                affine(coarse[0:32, par, :].bitcast(F32R), acc[0:32, par, :],
                       scale=col[0:32, MASK_QK:MASK_QK + 1]).then_inc(theta_coarse, 1)
                act.wait_ge(pool_done, b * NCH + (c + 1))
                affine(coarse[C:96, par, 0:P].bitcast(F32R), pooled[C:96, bass.ds(c * P, P)],
                       scale=col[C:96, MASK_QK:MASK_QK + 1]).then_inc(phi_coarse, 1)
                if isinstance(c, int) and c == 1:
                    act.wait_ge(in0_used, b * NCH + 1)
                    stage(b, 0, 0, 0)

            def conv1_out(b, c):
                act.wait_ge(conv1_ready, b * NCH + c + 1)
                nc.scalar.activation(pc[:, chunk(c)], work[:, c % 2, :], ACT.Relu, bias=bn[:, 0, 5:6],
                                     scale=bn[:, 0, 4:5]).then_inc(pc_ready, 1)

            def qk_out(b, c):
                act.wait_ge(qk_ready, b * NCH + c + 1)
                if c >= 2:
                    act.wait_ge(qk_split, b * NCH + (c - 1))
                affine(coarse[0:C, c % 2, :].bitcast(F32R), work[0:C, 2 + c % 2, :],
                       scale=col[0:C, MASK_QK:MASK_QK + 1], bias=bqk_m[:, :]).then_inc(qk_coarse, 1)

            def conv2_out(b, c, par):
                second = early(c, 2) and not early(c, 1)
                if second:
                    features(b, c - 1, 1 - par)
                in0(b + 1, c, par)
                if not early(c, 2):
                    features(b, c - 1, 1 - par)
                act.wait_ge(conv2_ready, b * NCH + (c + 1))
                act.wait_ge(branch_sum, b * NCH + (c + 1))
                nc.scalar.copy(part[0:C, par, :], work[C:P, par, :])
                nc.scalar.copy(part[C:P, par, :], work[0:C, 2 + par, :]).then_inc(part_ready, 1)
                if early(c, 1):
                    copy_sum(b, 1, NCH - 1, 1)
                elif early(c, 2):
                    act.wait_ge(phi_split, b * NCH + (NCH + 1))
                    split_post(b, 1, NCH - 1, 1)

            def features(b, c, par):
                act.wait_ge(branch_sum, b * NCH + (c + 1 + 2))
                act.wait_ge(out_ready, b * NCH + (c + 1))
                nc.scalar.activation(feat[:, par, :], bsum[:, par, :], ACT.Relu, bias=bn[:, 1, 5:6],
                                     scale=bn[:, 1, 4:5]).then_inc(feat_ready, 1)

            def start0(b):
                act.wait_ge(in0_used, b * NCH + NCH)

            chunk_loop(act, lambda c, par: in0(0, c, par), 2, 0)
            start0(0)
            with act.Fori(0, B) as b:
                chunk_loop(act, lambda c, par: attend0(b, c, par), 2, 2)
                copy_sum(b, 0, NCH - 1, 1)
                conv1_out(b, 0)
                split_post(b, 0, NCH - 2, 0)
                conv1_out(b, 1)
                act.wait_ge(post_split, step_no(b, 0, NCH - 1) + 1)
                qk_out(b, 0)
                act.wait_ge(qk_split, b * NCH + 1)
                stage(b, 1, 0, 0)
                split_post(b, 0, NCH - 1, 1)
                act.wait_ge(post_split, step_no(b, 0, NCH) + 1)
                for c in range(2, NCH + 1):
                    if c < NCH:
                        conv1_out(b, c)
                    qk_out(b, c - 1)
                act.wait_ge(cam_step, b * 5 + 4)
                nc.scalar.activation(ex[:, :], en[:, :], ACT.Exp, bias=st[:, 2:3],
                                     accum_out=st[:, 3:4]).then_inc(cam_exp, 1)
                stage(b, 1, 1, 1)
                row(b, 1, 0, 0, 1)
                chunk_loop(act, lambda c, par: attend1(b, c, par), 1, 1)
                copy_num(b, NCH - 1)
                chunk_loop(act, lambda c, par: conv2_out(b, c, par), 2, 0)
                start0(b + 1)
                features(b, NCH - 1, 1)

        @block.vector
        def _(dve):
            v = nc.vector
            dve.sem_inc(max_done, 2)
            dve.sem_inc(num_taken, 1)
            dve.sem_inc(u_ready, 1)
            dve.sem_inc(oct_ready, 2)
            dve.sem_inc(sum_taken, 2)
            dve.sem_inc(post_split, 1)
            dve.sem_inc(branch_sum, 2)
            dve.sem_inc(out_staged, 2)
            v.memset(keys[:, :].bitcast(F32), 0.0).then_inc(keys_zero, 1)
            for t in (x_in[C:P, :], qs[:, :, :].bitcast(F32), mx_cols[:, :, :, :], wi0[C:P, :], wqk[C:P, :],
                      proj_y[96:P, :], cam_w[0:C, :], qall[32:C, :]):
                v.memset(t, 0.0)
            v.memset(ones[:, :], 1.0)
            v.memset(gt[:, :, 0:C2], 1.0)
            dve.wait_ge(keys_zero, 1)
            v.memset(keys[32:34, :].bitcast(F32), 1.0).then_inc(keys_zero, 1)
            dve.wait_ge(keys_zero, 2)
            dve.wait_ge(consts_in, 16 * N_LOADS)
            n_setup = 0

            def link(ins):
                nonlocal n_setup
                n_setup += 1
                ins.then_inc(setup_dve, 1)
                dve.wait_ge(setup_dve, n_setup)

            for k, (g, bb, m, var) in enumerate(((BN1_G, BN1_B, BN1_M, BN1_V), (BN2_G, BN2_B, BN2_M, BN2_V))):
                ins = v.tensor_scalar(bn[:, k, 0:1], col[:, var:var + 1], 1e-5, None, ALU.add)
            link(ins)
            dve.wait_ge(setup_act, 2)
            for k, (g, bb, m, var) in enumerate(((BN1_G, BN1_B, BN1_M, BN1_V), (BN2_G, BN2_B, BN2_M, BN2_V))):
                q = [bn[:, k, i:i + 1] for i in range(6)]
                link(v.reciprocal(q[2], q[1]))
                link(v.tensor_tensor(q[3], q[0], q[2], ALU.mult))
                link(v.tensor_tensor(q[3], q[3], q[1], ALU.add))
                link(v.tensor_scalar(q[3], q[3], 0.5, None, ALU.mult))
                link(v.reciprocal(q[2], q[3]))
                link(v.tensor_tensor(q[4], q[2], col[:, g:g + 1], ALU.mult))
                link(v.tensor_tensor(q[3], q[4], col[:, m:m + 1], ALU.mult))
                link(v.tensor_tensor(q[5], col[:, bb:bb + 1], q[3], ALU.subtract))
            v.tensor_scalar(neg_idn[:], idn[:], -1.0, None, ALU.mult)
            v.tensor_scalar(proj_y[C:96, :], proj_y[C:96, :], col[C:96, GAMMA0:GAMMA0 + 1], None, ALU.mult)
            v.tensor_scalar(proj_p[C:P, :], proj_p[C:P, :], col[C:P, GAMMA_PA:GAMMA_PA + 1], None, ALU.mult)
            link(v.tensor_tensor(bv_g[:, 0:1], col[:, B_V:B_V + 1], col[:, GAMMA_PA:GAMMA_PA + 1], ALU.mult))
            v.tensor_tensor(bv_g[:, 1:2], bv_g[:, 0:1], col[:, MASK_HALF:MASK_HALF + 1], ALU.mult)
            v.tensor_tensor(bqk_m[:, :], col[0:C, B_QK:B_QK + 1], col[0:C, MASK_QK:MASK_QK + 1], ALU.mult)
            c1 = wtmp[:, 0:TAPS * P].rearrange("p (t m) -> p t m", t=TAPS)
            link(v.tensor_copy(w1[:, 0, :, :], c1))
            link(v.tensor_tensor(w1[:, 1, :, :], c1, w1[:, 0, :, :].bitcast(F32), ALU.subtract))
            for w, off, hi in ((w2p, TAPS * P, 0), (w2c, TAPS * (P + C), 1)):
                src = wtmp[:, off:off + TAPS * C].rearrange("p (t m) -> p t m", t=TAPS)
                a, f = w[:, :, hi * C:(hi + 1) * C], w[:, :, (1 - hi) * C:(2 - hi) * C]
                link(v.tensor_copy(a, src))
                link(v.tensor_tensor(f, src, a.bitcast(F32), ALU.subtract))
            dve.sem_inc(consts_ready, 1)

            def take_max(b, layer, c, par, u, bank):
                n = TILES[layer] // QT
                lt, kc = u if isinstance(u, tuple) else (u // n, u % n)
                if isinstance(u, tuple):
                    u = kc * QT + lt
                dve.wait_ge(smax_ready, tile_no(b, layer, c, u + 1))
                v.tensor_reduce(mx[:, par, lt, kc:kc + 1], ring[:, bank, :] if isinstance(bank, int) else bank, AX.X, ALU.max).then_inc(max_done, 1)

            def finish_max(b, layer, c, par):
                n = TILES[layer] // QT
                at = step_no(b, layer, c) * 2
                dve.wait_ge(max_done, tile_no(b, layer, c + 1, 2))
                v.tensor_reduce(mx1[:, par, :], mx[:, par, :, 0:n], AX.X, ALU.max).then_inc(mx_step, 1)
                dve.wait_ge(mx_step, at + 1)
                v.tensor_copy(mx_cols[:, par, :, 0].bitcast(F32R), mx1[:, par, :]).then_inc(mx_step, 1)
                dve.wait_ge(mx_step, at + 2)
                v.tensor_tensor(mx_cols[:, par, :, 1], mx1[:, par, :], mx_cols[:, par, :, 0],
                                ALU.subtract).then_inc(mx_ready, 1)

            def add_quads(b, c, j):
                dve.wait_ge(quad_ready, b * (NCH * GROUPS) + (c * GROUPS + 2 * j + 2 + 2))
                if j % 2 == 0:
                    dve.wait_ge(ones_done, b * (NCH * 2) + (c * 2 + j // 2 + 1))
                q = 2 * j % 4
                v.tensor_tensor(octs[:, j, :], quads[:, q, :], quads[:, q + 1, :], ALU.add).then_inc(oct_ready, 1)

            def take_num(b, c):
                dve.wait_ge(num_half, b * NCH + (c + 1))
                dve.wait_ge(u_ready, step_no(b, 1, c) + 1)
                v.tensor_tensor(wnum[C:P, :], acc[0:C, 0, :], half_num[:, :], ALU.add).then_inc(num_taken, 1)

            def take_sum(b, layer, c, par):
                dve.wait_ge(sum_half, step_no(b, layer, c) + 1)
                dve.wait_ge(u_ready, step_no(b, layer, c) + 1)
                v.tensor_tensor(sums[:, :], acc[0:C, par if layer == 0 else 1, :], half_sum[:, :],
                                ALU.add).then_inc(sum_taken, 1)

            def normalise(b, layer, c, stages=(0, 1, 2, 3)):
                n = (C2, C)[layer]
                lo, hi = n, 2 * n
                at = step_no(b, layer, c) * 3
                if 0 in stages:
                    dve.wait_ge(sum_taken, step_no(b, layer, c) + 1 + 2)
                    v.transpose(inv_t[0:n, :], sums[0:n, :]).then_inc(norm_step, 1)
                if 1 in stages:
                    dve.wait_ge(norm_step, at + 1)
                    v.reciprocal(inv_c[lo:hi, :], inv_t[0:n, 0:CHUNK:32]).then_inc(norm_step, 1)
                if 2 in stages:
                    dve.wait_ge(norm_step, at + 2)
                    v.transpose(inv[lo:hi, :].rearrange("p (a b) -> p a b", b=32),
                                inv_c[lo:hi, :].unsqueeze(2).to_broadcast([n, CHUNK // 32, 32])).then_inc(norm_step, 1)
                if 3 in stages and layer == 1:
                    dve.wait_ge(norm_step, at + 3)
                    dve.wait_ge(num_taken, b * NCH + (c + 1 + 1))
                    v.tensor_tensor(pc[C:P, chunk(c)], wnum[lo:hi, :], inv[lo:hi, :], ALU.mult).then_inc(u_ready, 1)

            def split_post(b, layer, c, odd):
                dve.wait_ge(post_coarse, step_no(b, layer, c) + 1)
                o = image_rows(y_pad, c)
                i, g = (a.rearrange("p (r w) -> p r w", w=W) for a in (post_out(layer, c, odd), coarse[:, 0, :]))
                if layer == 0:
                    v.tensor_tensor(o, i, g, ALU.subtract).then_inc(post_split, 1)
                else:
                    v.scalar_tensor_tensor(out=o, in0=i, scalar=bv_g[:, 0:1], in1=g, op0=ALU.add,
                                           op1=ALU.subtract).then_inc(post_split, 1)

            def attend0(b, c, par):
                nxt = not is_last(c)

                def units(*us):
                    for u in us:
                        if nxt:
                            take_max(b, 0, c + 1, 1 - par, u, ring_bank0(u, par))
                def before(stage):
                    if not early(c, 2):
                        normalise(b, 0, c - 2, (stage,))
                before(0)
                if not early(c, 3):
                    split_post(b, 0, c - 3, 1 - par)
                units(0)
                before(1)
                before(2)
                units(1, 2)
                if not early(c, 1):
                    take_sum(b, 0, c - 1, 1 - par)
                units(3, 4, 5, 6, 7)
                if nxt:
                    finish_max(b, 0, c + 1, 1 - par)
                else:
                    normalise(b, 0, c - 1)

            def attend1(b, c, par):
                nxt, before = not is_last(c), not early(c, 1)
                for u in range(FIRST_UNIT[GROUPS]):
                    if nxt:
                        take_max(b, 1, c + 1, 1 - par, u, ring_bank(u))
                    if u in OCT_UNITS:
                        add_quads(b, c, OCT_UNITS.index(u))
                    if before:
                        if u == NUM_UNIT:
                            take_num(b, c - 1)
                        if u == LAST_OCT_UNIT:
                            add_quads(b, c - 1, 3)
                        if u == SUM_UNIT:
                            take_sum(b, 1, c - 1, 1 - par)
                        for stage, at in enumerate(NORM_UNITS):
                            if u == at:
                                normalise(b, 1, c - 1, (stage,))
                        if u == POST_UNIT:
                            split_post(b, 1, c - 1, 1 - par)
                    elif u == NUM_UNIT:
                        dve.wait_ge(attn_t_ready, b + 1)
                        v.tensor_tensor(cam_w[C:P, :], acc[C:P, 1, 0:P], two_idn[C:P, :], ALU.add)\
                            .then_inc(cam_w_ready, 1)
                    if u == CAM_UNIT:
                        dve.wait_ge(cam_coarse, b * NCH + (c + 1))
                        v.tensor_tensor(image_rows(c_pad, c), ring_bank("cam").rearrange("p (r w) -> p r w", w=W),
                                        coarse[:, 1, :].rearrange("p (r w) -> p r w", w=W),
                                        ALU.subtract).then_inc(cam_split, 1)
                if nxt:
                    finish_max(b, 1, c + 1, 1 - par)
                add_quads(b, c, 2)

            def branch(b, c, par):
                if early(c, 1):
                    add_quads(b, NCH - 1, 3)
                in0(b + 1, c, par)
                if not early(c, 2):
                    stage_out(b, c - 2, par)
                if is_last(c):
                    stage_out(b, c - 1, 1 - par)
                dve.wait_ge(part_ready, b * NCH + (c + 1))
                dve.wait_ge(feat_ready, b * NCH + (c + 1))
                v.tensor_tensor(bsum[0:C, par, :], work[0:C, par, :], part[0:C, par, :], ALU.add)
                v.tensor_tensor(bsum[C:P, par, :], work[C:P, 2 + par, :], part[C:P, par, :],
                                ALU.add).then_inc(branch_sum, 1)
                if early(c, 1):
                    take_sum(b, 1, NCH - 1, 1)
                    normalise(b, 1, NCH - 1)
                elif early(c, 2):
                    split_post(b, 1, NCH - 1, 1)

            def first_max0(b, u):
                take_max(b, 0, 0, 0, (u % QT, u // QT), u % 2)

            def stage_out(b, c, par):
                dve.wait_ge(out_ready, b * NCH + (c + 1 + 2))
                dve.wait_ge(out_stored[par], b * (8 * NCH) + (c * 8 + (8 if par else 16)) )
                v.tensor_scalar(ostage[:, par, :], ring[0:C, par, :], col[0:C, B_OUT:B_OUT + 1], None,
                                ALU.add).then_inc(out_staged, 1)

            def in0(b, c, par):
                dve.wait_ge(in0_ready, b * NCH + (c + 1))
                v.tensor_reduce(pooled[C:P, bass.ds(c * P, P)].rearrange("p (a k) -> p a k", a=ROWS // 2),
                                acc[C:P, par, :].rearrange("p (a r k q) -> p a k r q", a=ROWS // 2, r=2, q=2),
                                AX.XY, ALU.max).then_inc(pool_done, 1)
                dve.wait_ge(theta_coarse, b * NCH + (c + 1))
                v.tensor_tensor(qall[0:32, chunk(c)].bitcast(F32R), acc[0:32, par, :], coarse[0:32, par, :],
                                ALU.subtract).then_inc(in0_used, 1)
                dve.wait_ge(phi_coarse, b * NCH + (c + 1))
                v.tensor_tensor(keys[0:32, bass.ds(c * P, P)], pooled[C:96, bass.ds(c * P, P)],
                                coarse[C:96, par, 0:P], ALU.subtract).then_inc(phi_split, 1)

            def start0(b, output=None):
                for u in range(TILES[0]):
                    if u == 2 and output:
                        output()
                    first_max0(b, u)
                finish_max(b, 0, 0, 0)
                dve.wait_ge(gt_ready, b + 1)
                v.tensor_copy(gt[:, :, C2:2 * C2], acc[:, 0, 0:TILES[0] * 32].rearrange("p (t c) -> p t c", c=32))\
                    .then_inc(gt_copied, 1)

            chunk_loop(dve, lambda c, par: in0(0, c, par), 2, 0)
            start0(0)
            with dve.Fori(0, B) as b:
                chunk_loop(dve, lambda c, par: attend0(b, c, par), 3, 1)
                split_post(b, 0, NCH - 3, 1)
                take_sum(b, 0, NCH - 1, 1)
                normalise(b, 0, NCH - 1)
                split_post(b, 0, NCH - 2, 0)

                def qk_out(c):
                    dve.wait_ge(qk_coarse, b * NCH + c + 1)
                    for o, r in ((qall[0:32, chunk(c)].bitcast(F32R), slice(0, 32)), (keys[0:32, chunk(c)], slice(32, C))):
                        last = v.scalar_tensor_tensor(out=o, in0=work[r, 2 + c % 2, :], scalar=col[r, B_QK:B_QK + 1],
                                                      in1=coarse[r, c % 2, :], op0=ALU.add, op1=ALU.subtract)
                    last.then_inc(qk_split, 1)

                def transposed(c):
                    dve.wait_ge(tr_ready, b * NCH + c + 1)
                    v.tensor_copy(pt_ct[:, QT * c:QT * (c + 1), :],
                                  acc[:, 1, :].rearrange("p (t c) -> p t c", t=QT)).then_inc(tr_copied, 1)

                qk_out(0)
                transposed(0)
                split_post(b, 0, NCH - 1, 1)
                for c in range(2, NCH + 1):
                    ahead = QT if c < NCH else 2
                    for lt in range(ahead):
                        take_max(b, 1, 0, 0, (lt, c - 2), lt % 2)
                    qk_out(c - 1)
                    transposed(c - 1)
                    for lt in range(ahead, QT):
                        take_max(b, 1, 0, 0, (lt, c - 2), lt % 2)
                e = acc[0:C, 0, 0:C]
                last_keys = NCH - 1
                dve.wait_ge(energy_ready, b + 1)
                v.tensor_reduce(st[:, 0:1], e, AX.X, ALU.max).then_inc(cam_step, 1)
                take_max(b, 1, 0, 0, (0, last_keys), 0)
                dve.wait_ge(cam_step, b * 5 + 1)
                v.tensor_scalar(en[:, :], e, st[:, 0:1], -1.0, ALU.subtract, ALU.mult).then_inc(cam_step, 1)
                take_max(b, 1, 0, 0, (1, last_keys), 1)
                dve.wait_ge(cam_step, b * 5 + 2)
                v.tensor_reduce(st[:, 1:2], en[:, :], AX.X, ALU.max).then_inc(cam_step, 1)
                take_max(b, 1, 0, 0, (2, last_keys), 0)
                dve.wait_ge(cam_step, b * 5 + 3)
                v.tensor_scalar(st[:, 2:3], st[:, 1:2], -1.0, None, ALU.mult).then_inc(cam_step, 1)
                take_max(b, 1, 0, 0, (3, last_keys), 1)
                finish_max(b, 1, 0, 0)
                dve.wait_ge(cam_exp, b + 1)
                v.reciprocal(st[:, 4:5], st[:, 3:4]).then_inc(cam_step, 1)
                dve.wait_ge(cam_step, b * 5 + 5)
                for k in range(2):
                    last = v.tensor_scalar(attn[:, k, :], ex[:, :], st[:, 4:5],
                                           col[0:C, GAMMA_CA:GAMMA_CA + 1], ALU.mult, ALU.mult)
                last.then_inc(attn_ready, 1)
                chunk_loop(dve, lambda c, par: attend1(b, c, par), 1, 1)
                take_num(b, NCH - 1)
                chunk_loop(dve, lambda c, par: branch(b, c, par), 2, 2)
                start0(b + 1, lambda: stage_out(b, NCH - 1, 1))


N_LOADS = 18


def kernel(**inputs):
    import numpy as np
    import concourse.bacc as bacc
    from concourse.bass_utils import run_bass_kernel_spmd

    g = {k: np.ascontiguousarray(v) for k, v in inputs.items()}
    f = np.float32

    def l1(name):
        return g["L1_conv_" + name]

    zero = np.zeros((C, 32), f)
    w_in0 = np.concatenate([np.tile(g["L0_conv_w_theta"].T, (1, 4)), zero, np.tile(g["L0_conv_w_phi"].T, (1, 4)),
                            g["L0_conv_w_g"].T], axis=1)
    w_o0 = np.tile(g["L0_conv_w_o"].T, (1, 2))
    w_qk = np.concatenate([np.tile(l1("wq").T, (1, 4)), np.tile(l1("wk").T, (1, 4))], axis=1)
    w_v = np.tile(l1("wv").T, (1, 2))

    def taps(w):
        return w.transpose(1, 2, 3, 0).reshape(C, TAPS, C)

    w_c1 = np.tile(np.concatenate([taps(l1("w_pam1")), taps(l1("w_cam1"))], axis=2), (2, 1, 1)).reshape(P, TAPS * P)
    w_c2p = np.tile(taps(l1("w_pam2")), (2, 1, 1)).reshape(P, TAPS * C)
    w_c2c = np.tile(taps(l1("w_cam2")), (2, 1, 1)).reshape(P, TAPS * C)
    w_out = np.tile(l1("w_out").T, (2, 1))
    cols = np.zeros((P, NCOL), f)
    for k, n in ((0, "1"), (4, "2")):
        for i, s in enumerate("gbmv"):
            cols[:, k + i] = np.concatenate([l1(f"bn_pam{n}_{s}"), l1(f"bn_cam{n}_{s}")])
    cols[:C, B_QK] = np.concatenate([np.tile(l1("bq"), 4), np.tile(l1("bk"), 4)])
    cols[:, B_V] = np.tile(l1("bv"), 2)
    cols[:C, B_OUT] = l1("b_out")
    cols[:, GAMMA0] = g["L0_conv_gamma"]
    cols[:, GAMMA_PA] = l1("gamma_pa")
    cols[:, GAMMA_CA] = l1("gamma_ca")
    cols[C:, MASK_HALF] = 1
    group = np.arange(32) // C8
    cols[:32, MASK_QK] = group // 2
    cols[32:64, MASK_QK] = group % 2
    cols[64:96, MASK_QK] = group % 2
    arrays = {"x": g["x"].reshape(B, C, L), "cols": cols, "ident": np.eye(P, dtype=f), "w_in0": w_in0, "w_o0": w_o0,
              "w_qk": w_qk, "w_v": w_v, "w_c1": w_c1, "w_c2p": w_c2p, "w_c2c": w_c2c, "w_out": w_out}
    arrays = {f"in_{k}": np.ascontiguousarray(a) for k, a in arrays.items()}
    nc = bacc.Bacc("TRN2", target_bir_lowering=False, num_devices=1)
    args = [nc.dram_tensor(k, a.shape, mybir.dt.from_np(a.dtype), kind="ExternalInput").ap() for k, a in arrays.items()]
    args.append(nc.dram_tensor("out_0", (B, C, L), F32, kind="ExternalOutput").ap())
    build(nc, *args)
    r = run_bass_kernel_spmd(nc, [arrays], core_ids=[0])
    return r.results[0]["out_0"].reshape(B, C, H, W)
```
